# Optimizing a Trainium2 kernel written in Bass

```python
import numpy as np
import jax
import jax.numpy as jnp

def _softmax(x, axis=-1):
    return jax.nn.softmax(x, axis=axis)

def _gelu(x):
    return jax.nn.gelu(x, approximate=True)

def _silu(x):
    return jax.nn.silu(x)

def _sigmoid(x):
    return jax.nn.sigmoid(x)

def _layernorm(x, axis=-1, eps=1e-05):
    m = jnp.mean(x, axis=axis, keepdims=True)
    v = jnp.var(x, axis=axis, keepdims=True)
    return (x - m) / jnp.sqrt(v + eps)

def _scatter_add(tgt, idx, src, axis=0):
    return tgt.at[idx].add(src)

def _segment_sum(src, seg, n):
    return jax.ops.segment_sum(src, seg, n)
kernel_name = 'mk_hybrid_d1_jaxref_r4_a1b8cd'

def setup_inputs(seed: int=0):
    np.random.seed(seed)
    _w = jnp.asarray

    def _L0_attn_a_setup():
        import jax, jax.numpy as jnp
        import numpy as np
        DIM = 256
        H = 16
        HD = DIM // H
        EPS_DENOM = 1e-06
        EPS_LN = 1e-05
        key = jax.random.key(seed)
        ks = jax.random.split(key, 8)
        B, N = (4, 1024)
        s = 1.0 / np.sqrt(DIM)
        return {'x': jax.random.normal(ks[0], (B, N, DIM), dtype=jnp.float32), 'Wq': jax.random.normal(ks[1], (DIM, DIM), dtype=jnp.float32) * s, 'bq': jnp.zeros((DIM,), dtype=jnp.float32), 'Wk': jax.random.normal(ks[2], (DIM, DIM), dtype=jnp.float32) * s, 'bk': jnp.zeros((DIM,), dtype=jnp.float32), 'Wv': jax.random.normal(ks[3], (DIM, DIM), dtype=jnp.float32) * s, 'bv': jnp.zeros((DIM,), dtype=jnp.float32), 'gamma': jnp.ones((DIM,), dtype=jnp.float32), 'beta': jnp.zeros((DIM,), dtype=jnp.float32)}
    _L0_attn_a_in = _L0_attn_a_setup()

    def _L0_attn_b_setup():
        import math
        import jax, jax.numpy as jnp
        import numpy as np
        NUM_BUCKETS = 32
        MAX_DISTANCE = 128
        HEADS = 8
        DIM_HEAD = 64

        def _relative_position_bucket(rel_pos, num_buckets=NUM_BUCKETS, max_distance=MAX_DISTANCE):
            n = jnp.maximum(-rel_pos, 0)
            max_exact = num_buckets // 2
            is_small = n < max_exact
            val_if_large = max_exact + (jnp.log(jnp.maximum(n, 1).astype(jnp.float32) / max_exact) / math.log(max_distance / max_exact) * (num_buckets - max_exact)).astype(jnp.int32)
            val_if_large = jnp.minimum(val_if_large, num_buckets - 1)
            return jnp.where(is_small, n, val_if_large)
        key = jax.random.key(seed)
        ks = jax.random.split(key, 5)
        b, n, dim = (2, 512, 256)
        inner = HEADS * DIM_HEAD
        return {'x': jax.random.normal(ks[0], (b, n, dim), dtype=jnp.float32), 'Wq': jax.random.normal(ks[1], (dim, inner), dtype=jnp.float32) * dim ** (-0.5), 'Wkv': jax.random.normal(ks[2], (dim, 2 * inner), dtype=jnp.float32) * dim ** (-0.5), 'Wo': jax.random.normal(ks[3], (inner, dim), dtype=jnp.float32) * inner ** (-0.5), 'bo': jnp.zeros((dim,), dtype=jnp.float32), 'rel_emb': jax.random.normal(ks[4], (NUM_BUCKETS, HEADS), dtype=jnp.float32) * 0.02}
    _L0_attn_b_in = _L0_attn_b_setup()

    def _L0_ffn_setup():
        import jax, jax.numpy as jnp
        import numpy as np
        B, S, D = (2, 256, 256)
        E, K, F, FS = (8, 2, 128, 256)
        key = jax.random.key(seed)
        ks = jax.random.split(key, 9)
        s = lambda k, shape, fan: jax.random.normal(k, shape, jnp.float32) * fan ** (-0.5)
        return {'x': jax.random.normal(ks[0], (B, S, D), jnp.float32), 'Wr': s(ks[1], (D, E), D), 'Wg': s(ks[2], (E, D, F), D), 'Wu': s(ks[3], (E, D, F), D), 'Wd': s(ks[4], (E, F, D), F), 'Sg': s(ks[5], (D, FS), D), 'Su': s(ks[6], (D, FS), D), 'Sd': s(ks[7], (FS, D), FS), 'expert_bias': jnp.zeros((E,), jnp.float32)}
    _L0_ffn_in = _L0_ffn_setup()
    _d = {'L0_attn_a_x': _L0_attn_a_in['x'], 'L0_attn_a_Wq': _L0_attn_a_in['Wq'], 'L0_attn_a_bq': _L0_attn_a_in['bq'], 'L0_attn_a_Wk': _L0_attn_a_in['Wk'], 'L0_attn_a_bk': _L0_attn_a_in['bk'], 'L0_attn_a_Wv': _L0_attn_a_in['Wv'], 'L0_attn_a_bv': _L0_attn_a_in['bv'], 'L0_attn_a_gamma': _L0_attn_a_in['gamma'], 'L0_attn_a_beta': _L0_attn_a_in['beta'], 'L0_attn_b_Wq': _L0_attn_b_in['Wq'], 'L0_attn_b_Wkv': _L0_attn_b_in['Wkv'], 'L0_attn_b_Wo': _L0_attn_b_in['Wo'], 'L0_attn_b_bo': _L0_attn_b_in['bo'], 'L0_attn_b_rel_emb': _L0_attn_b_in['rel_emb'], 'L0_ffn_Wr': _L0_ffn_in['Wr'], 'L0_ffn_Wg': _L0_ffn_in['Wg'], 'L0_ffn_Wu': _L0_ffn_in['Wu'], 'L0_ffn_Wd': _L0_ffn_in['Wd'], 'L0_ffn_Sg': _L0_ffn_in['Sg'], 'L0_ffn_Su': _L0_ffn_in['Su'], 'L0_ffn_Sd': _L0_ffn_in['Sd'], 'L0_ffn_expert_bias': _L0_ffn_in['expert_bias']}
    _x0 = _d['L0_attn_a_x']
    _d['L0_attn_a_x'] = jax.random.normal(jax.random.fold_in(jax.random.key(seed), 1), (4, 1024, 256), dtype=_x0.dtype)
    del _x0
    return _d

def reference(L0_attn_a_x, L0_attn_a_Wq, L0_attn_a_bq, L0_attn_a_Wk, L0_attn_a_bk, L0_attn_a_Wv, L0_attn_a_bv, L0_attn_a_gamma, L0_attn_a_beta, L0_attn_b_Wq, L0_attn_b_Wkv, L0_attn_b_Wo, L0_attn_b_bo, L0_attn_b_rel_emb, L0_ffn_Wr, L0_ffn_Wg, L0_ffn_Wu, L0_ffn_Wd, L0_ffn_Sg, L0_ffn_Su, L0_ffn_Sd, L0_ffn_expert_bias):

    def _L0_attn_a_ref(x, Wq, bq, Wk, bk, Wv, bv, gamma, beta):
        import jax, jax.numpy as jnp
        import numpy as np
        DIM = 256
        H = 16
        HD = DIM // H
        EPS_DENOM = 1e-06
        EPS_LN = 1e-05
        B, N, C = x.shape
        q = (x @ Wq.T + bq).reshape(B, N, H, HD)
        k = (x @ Wk.T + bk).reshape(B, N, H, HD)
        v = (x @ Wv.T + bv).reshape(B, N, H, HD)
        q = jax.nn.relu(q)
        k = jax.nn.relu(k)
        kv = jnp.einsum('bnhd,bnhp->bhdp', k, v)
        k_sum = k.sum(axis=1)
        denom = jnp.einsum('bnhd,bhd->bnh', q, k_sum)
        denom = jnp.maximum(denom, EPS_DENOM)[..., None]
        ctx = jnp.einsum('bnhd,bhdp->bnhp', q, kv)
        out = (ctx / denom).reshape(B, N, C)
        y = out + x
        mu = y.mean(axis=-1, keepdims=True)
        var = y.var(axis=-1, keepdims=True)
        return (y - mu) / jnp.sqrt(var + EPS_LN) * gamma + beta

    def _L0_attn_b_ref(x, Wq, Wkv, Wo, bo, rel_emb):
        import math
        import jax, jax.numpy as jnp
        import numpy as np
        NUM_BUCKETS = 32
        MAX_DISTANCE = 128
        HEADS = 8
        DIM_HEAD = 64

        def _relative_position_bucket(rel_pos, num_buckets=NUM_BUCKETS, max_distance=MAX_DISTANCE):
            n = jnp.maximum(-rel_pos, 0)
            max_exact = num_buckets // 2
            is_small = n < max_exact
            val_if_large = max_exact + (jnp.log(jnp.maximum(n, 1).astype(jnp.float32) / max_exact) / math.log(max_distance / max_exact) * (num_buckets - max_exact)).astype(jnp.int32)
            val_if_large = jnp.minimum(val_if_large, num_buckets - 1)
            return jnp.where(is_small, n, val_if_large)
        b, n, dim = x.shape
        h, d = (HEADS, DIM_HEAD)
        scale = d ** (-0.5)
        bias_scale = d ** 0.5
        q = x @ Wq
        kv = x @ Wkv
        k, v = jnp.split(kv, 2, axis=-1)

        def to_heads(t):
            return t.reshape(b, n, h, d).transpose(0, 2, 1, 3)
        q, k, v = (to_heads(q) * scale, to_heads(k), to_heads(v))
        sim = jnp.einsum('bhid,bhjd->bhij', q, k)
        pos = jnp.arange(n)
        rel_pos = pos[None, :] - pos[:, None]
        buckets = _relative_position_bucket(rel_pos)
        bias = rel_emb[buckets]
        bias = bias.transpose(2, 0, 1)[None] * bias_scale
        sim = sim + bias
        causal_mask = jnp.triu(jnp.ones((n, n), dtype=bool), k=1)
        sim = jnp.where(causal_mask, -jnp.finfo(sim.dtype).max, sim)
        attn = jax.nn.softmax(sim, axis=-1)
        out = jnp.einsum('bhij,bhjd->bhid', attn, v)
        out = out.transpose(0, 2, 1, 3).reshape(b, n, h * d)
        return out @ Wo + bo

    def _L0_ffn_ref(x, Wr, Wg, Wu, Wd, Sg, Su, Sd, expert_bias):
        import jax, jax.numpy as jnp
        import numpy as np
        B, S, D = (2, 256, 256)
        E, K, F, FS = (8, 2, 128, 256)
        b, s, d = x.shape
        xf = x.reshape(-1, d)
        T = xf.shape[0]
        logits = xf @ Wr + expert_bias
        top_v, top_i = jax.lax.top_k(logits, K)
        probs = jax.nn.softmax(top_v, axis=-1)
        rw = jnp.zeros_like(logits).at[jnp.arange(T)[:, None], top_i].set(probs)
        gate = jnp.einsum('td,edf->tef', xf, Wg)
        up = jnp.einsum('td,edf->tef', xf, Wu)
        h = jax.nn.silu(gate) * up
        eo = jnp.einsum('tef,efd->ted', h, Wd)
        out = jnp.einsum('te,ted->td', rw, eo)
        out = out + jax.nn.silu(xf @ Sg) * (xf @ Su) @ Sd
        return out.reshape(b, s, d)
    x = L0_attn_a_x
    x = x + _L0_attn_a_ref(_layernorm(x, axis=-1), L0_attn_a_Wq, L0_attn_a_bq, L0_attn_a_Wk, L0_attn_a_bk, L0_attn_a_Wv, L0_attn_a_bv, L0_attn_a_gamma, L0_attn_a_beta)
    x = x + _L0_ffn_ref(_layernorm(x, axis=-1), L0_ffn_Wr, L0_ffn_Wg, L0_ffn_Wu, L0_ffn_Wd, L0_ffn_Sg, L0_ffn_Su, L0_ffn_Sd, L0_ffn_expert_bias)
    x = x + _L0_attn_b_ref(_layernorm(x, axis=-1), L0_attn_b_Wq, L0_attn_b_Wkv, L0_attn_b_Wo, L0_attn_b_bo, L0_attn_b_rel_emb)
    x = x + _L0_ffn_ref(_layernorm(x, axis=-1), L0_ffn_Wr, L0_ffn_Wg, L0_ffn_Wu, L0_ffn_Wd, L0_ffn_Sg, L0_ffn_Su, L0_ffn_Sd, L0_ffn_expert_bias)
    return x

_drawn_inputs = setup_inputs


def setup_inputs(seed=0):
    import zlib

    import numpy as np

    out = dict(_drawn_inputs(seed))
    spreads = {'L0_attn_a_bq': (0.0, 2.0),
     'L0_attn_a_bk': (0.0, 2.0),
     'L0_attn_a_bv': (0.0, 0.1),
     'L0_attn_a_gamma': (1.0, 0.2),
     'L0_attn_a_beta': (0.0, 0.1),
     'L0_attn_b_bo': (0.0, 0.1),
     'L0_ffn_expert_bias': (0.0, 0.1)}
    factors = {'L0_attn_b_rel_emb': 5.368}
    for name, (base, spread) in spreads.items():
        noise = np.random.default_rng([zlib.crc32(name.encode()), seed]).standard_normal(out[name].shape)
        drawn = base * np.exp(spread * noise) if base else spread * noise
        out[name] = jnp.asarray(drawn.astype(out[name].dtype))
    for name, factor in factors.items():
        out[name] = (out[name] * factor).astype(out[name].dtype)
    return out
```

```python
import math
from contextlib import ExitStack

import numpy as np

import concourse.bass as bass
from concourse import mybir

F32 = mybir.dt.float32
F32R = mybir.dt.float32r
U32 = mybir.dt.uint32
ALU = mybir.AluOpType
ACT = mybir.ActivationFunctionType
AX = mybir.AxisListType

P = 128
D = 256
DB = D // P
B, N = 4, 1024
T = B * N // P
CT = 4
CW = CT * P
NCH = T // CT
EPS_LN = 1e-5

E, F, FS = 8, 128, 256
NSH = FS // F
NFB = NSH + E
FBW = 2 * D + D


def dyn(i, size=1):
    return slice(i, i + size) if isinstance(i, int) else bass.ds(i, size)


def loop(nc, eng, start, end):
    return nc.Fori(start, end, engines=[eng.engine], hint_back_edge=True)


def wait_apart(nc, eng, c, sem, value):
    eng.wait_ge(sem, value)
    nc.vector.memset(c.carrier[:], 0.0)


class Mem:

    def __init__(self, nc, ctx, tag):
        self.nc, self.ctx, self.tag, self.sems = nc, ctx, tag, []

    def sb(self, name, shape, dt=F32):
        return self.ctx.enter_context(self.nc.sbuf_tensor(f"{self.tag}_{name}", shape, dt))

    def ps(self, name, shape, dt=F32):
        return self.ctx.enter_context(self.nc.psum_tensor(f"{self.tag}_{name}", shape, dt))

    def sem(self, name):
        self.sems.append(self.nc.alloc_semaphore(name=f"{self.tag}_{name}"))
        return self.sems[-1]

    def clear_sems(self):
        self.nc.clear_and_free_semaphores(self.sems)
        self.nc.all_engine_barrier()


def ffn_stage(nc, tag, x_sb, c, dram, out_view=None):
    with ExitStack() as ctx:
        m = Mem(nc, ctx, tag)
        RAW = 4
        w_raw = m.sb("w_raw", [P, RAW, FBW])
        w_hi = m.sb("w_hi", [P, NFB, FBW], F32R)
        w_lo = m.sb("w_lo", [P, NFB, FBW], F32R)
        wr_raw = m.sb("wr_raw", [P, DB, E])
        wr_hi = m.sb("wr_hi", [P, DB, E], F32R)
        wr_lo = m.sb("wr_lo", [P, DB, E], F32R)
        ebias = m.sb("ebias", [E, 1])
        stats = m.sb("stats", [P, CT, 6])
        mv = m.sb("mv", [P, CT, 2])
        veps = m.sb("veps", [P, CT])
        rstd = m.sb("rstd", [P, CT])
        mr = m.sb("mr", [P, CT])
        nmr = m.sb("nmr", [P, CT])
        carrier = m.sb("carrier", [P, 1])
        xn = m.sb("xn", [P, CT, D])
        xt_hi = m.sb("xt_hi", [P, 2, DB, CW], F32R)
        xt_lo = m.sb("xt_lo", [P, 2, DB, CW], F32R)
        lg = m.sb("lg", [E, CW])
        top = m.sb("top", [P, CT, 8])
        topi = m.sb("topi", [P, CT, 8], U32)
        topf = m.sb("topf", [P, CT, 2])
        gap = m.sb("gap", [P, CT])
        th = m.sb("th", [P, CT])
        prob = m.sb("prob", [P, CT, 2])
        hot1 = m.sb("hot1", [P, CT, E])
        hot2 = m.sb("hot2", [P, CT, E])
        pr1 = m.sb("pr1", [P, CT, E])
        pr2 = m.sb("pr2", [P, CT, E])
        rw = m.sb("rw", [P, CT, E])
        rwt = m.sb("rwt", [E, CW])
        rw_row = m.sb("rw_row", [1, E, CW])
        rw_bc = m.sb("rw_bc", [P, E, CW])
        sil = m.sb("sil", [P, 2, CW])
        su = m.sb("su", [P, 2, CW])
        hid = m.sb("hid", [P, 2, CW])
        h_hi = m.sb("h_hi", [P, 5, CW], F32R)
        h_lo = m.sb("h_lo", [P, 5, CW], F32R)
        ot = m.sb("ot", [P, DB, CW])
        g_ps = [m.ps(f"g{i}", [P, CW]) for i in range(2)]
        u_ps = [m.ps(f"u{i}", [P, CW]) for i in range(2)]
        o_ps = [m.ps(f"o{i}", [P, CW]) for i in range(DB)]
        t_ps = [m.ps(f"t{i}", [P, CW]) for i in range(2)]

        w_in = [m.sem(f"w_in{i}") for i in range(NFB)]
        wr_in, wr_hi_done, wr_lo_done = m.sem("wr_in"), m.sem("wr_hi_done"), m.sem("wr_lo_done")
        w_hi_done, w_lo_done = m.sem("w_hi_done"), m.sem("w_lo_done")
        stats_done, mv_done = m.sem("stats_done"), m.sem("mv_done")
        pool_step, rstd_done, xn_done = m.sem("pool_step"), m.sem("rstd_done"), m.sem("xn_done")
        xt_ready, xt_hi_done, xt_lo_done = m.sem("xt_ready"), m.sem("xt_hi_done"), m.sem("xt_lo_done")
        lg_ready, lg_done, lgt_ready = m.sem("lg_ready"), m.sem("lg_done"), m.sem("lgt_ready")
        top_done, dve_step, gap_done, th_done = m.sem("top_done"), m.sem("dve_step"), m.sem("gap_done"), m.sem("th_done")
        rw_done, rwt_ready, rwt_done = m.sem("rw_done"), m.sem("rwt_ready"), m.sem("rwt_done")
        row_done, bc_done = m.sem("row_done"), m.sem("bc_done")
        g_ready, u_ready, sil_done, mul_done = m.sem("g_ready"), m.sem("u_ready"), m.sem("sil_done"), m.sem("mul_done")
        rwmul_done, hi_done, lo_done, down_done = m.sem("rwmul_done"), m.sem("hi_done"), m.sem("lo_done"), m.sem("down_done")
        ot0_done, ot1_done, back_ready, y_added = m.sem("ot0_done"), m.sem("ot1_done"), m.sem("back_ready"), m.sem("y_added")
        stored = m.sem("stored")

        def chunks(eng, body, tail):
            body(0, 0, True, False)
            with loop(nc, eng, 0, (NCH - 2) // 2) as i:
                body(i * 2 + 1, 1, False, False)
                body(i * 2 + 2, 0, False, False)
            body(NCH - 1, 1, False, True)
            tail()

        with nc.Block() as block:

            @block.sync
            def _(sp):
                for fb in range(NFB):
                    if fb >= RAW:
                        sp.wait_ge(w_lo_done, fb - RAW + 1)
                    sp.dma_start(w_raw[:, fb % RAW, :], dram["w_ffn"][fb]).then_inc(w_in[fb], 16)
                    if fb == 0:
                        sp.dma_start(wr_raw[:], dram["w_router"]).then_inc(wr_in, 16)
                        sp.dma_start(ebias[:], dram["expert_bias"]).then_inc(wr_in, 16)

                def row(n):
                    sp.wait_ge(rwt_done, n + 1)
                    if not isinstance(n, int) or n > 0:
                        sp.wait_ge(bc_done, n * E)
                    sp.dma_start(rw_row[0:1, :, :], rwt[:, :]).then_inc(row_done, 16)

                def store(n):
                    sp.wait_ge(y_added, n * 2 + 2)
                    sp.dma_start(out_view[:, dyn(n * CT, CT), :], x_sb[:, dyn(n * CT, CT), :]).then_inc(stored, 16)

                row(0)
                with loop(nc, sp, 0, NCH - 1) as i:
                    row(i + 1)
                    if out_view is not None:
                        store(i)
                if out_view is not None:
                    store(NCH - 1)
                    sp.wait_ge(stored, 16 * NCH)

            @block.tensor
            def _(pe):
                def transposes(n, par):
                    pe.wait_ge(xn_done, n * CT + CT)
                    for d in range(DB):
                        for j in range(CT):
                            last = nc.tensor.transpose(t_ps[d][:, j * P:(j + 1) * P], xn[:, j, d * P:(d + 1) * P], c.ident[:])
                        last.then_inc(xt_ready, 1)

                def router(n, par):
                    pe.wait_ge(xt_hi_done, n * DB + DB)
                    pe.wait_ge(xt_lo_done, n * DB + DB)
                    k = 0
                    for d in range(DB):
                        for w, xt in ((wr_hi, xt_hi), (wr_hi, xt_lo), (wr_lo, xt_hi)):
                            last = nc.tensor.matmul(t_ps[0][0:E, :], w[:, d, :], xt[:, par, d, :], start=(k == 0), stop=(k == 5))
                            k += 1
                    last.then_inc(lg_ready, 1)

                def logits_back(n):
                    for j in range(CT):
                        last = nc.tensor.transpose(t_ps[1][:, j * E:(j + 1) * E], lg[:, j * P:(j + 1) * P], c.ident[0:E, 0:E])
                    last.then_inc(lgt_ready, 1)

                def weights_over(n):
                    pe.wait_ge(rw_done, n + 1)
                    for j in range(CT):
                        last = nc.tensor.transpose(t_ps[0][0:E, j * P:(j + 1) * P], rw[:, j, :], c.ident[:])
                    last.then_inc(rwt_ready, 1)

                def gate_up(n, par, fb, first):
                    if first:
                        pe.wait_ge(w_hi_done, fb + 1)
                        pe.wait_ge(w_lo_done, fb + 1)
                    fresh = first and fb < 2
                    for ps, off, free, ready in ((g_ps, 0, sil_done, g_ready), (u_ps, F, mul_done, u_ready)):
                        if not fresh:
                            pe.wait_ge(free, n * NFB + (fb - 1))
                        k = 0
                        for d in range(DB):
                            lo = d * 2 * F + off
                            for w, xt in ((w_hi, xt_hi), (w_hi, xt_lo), (w_lo, xt_hi)):
                                last = nc.tensor.matmul(ps[fb % 2][:], w[:, fb, lo:lo + F], xt[:, par, d, :], start=(k == 0), stop=(k == 5))
                                k += 1
                        last.then_inc(ready, 1)

                def down(n, fb):
                    pe.wait_ge(hi_done, n * NFB + (fb + 1))
                    pe.wait_ge(lo_done, n * NFB + (fb + 1))
                    if fb == 0 and (not isinstance(n, int) or n > 0):
                        pe.wait_ge(ot0_done, n)
                        pe.wait_ge(ot1_done, n)
                    for d in range(DB):
                        lo = 2 * D + d * P
                        for k, (w, h) in enumerate(((w_hi, h_hi), (w_hi, h_lo), (w_lo, h_hi))):
                            last = nc.tensor.matmul(o_ps[d][:], w[:, fb, lo:lo + P], h[:, fb % 5, :],
                                                    start=(fb == 0 and k == 0), stop=(fb == NFB - 1 and k == 2))
                    last.then_inc(down_done, 1)

                def back(n):
                    pe.wait_ge(ot0_done, n + 1)
                    pe.wait_ge(ot1_done, n + 1)
                    for h in range(2):
                        for jj in range(2):
                            j = 2 * h + jj
                            for d in range(DB):
                                last = nc.tensor.transpose(t_ps[h][:, jj * D + d * P:jj * D + (d + 1) * P], ot[:, d, j * P:(j + 1) * P], c.ident[:])
                        last.then_inc(back_ready, 1)

                transposes(0, 0)
                pe.wait_ge(wr_hi_done, 1)
                pe.wait_ge(wr_lo_done, 1)
                router(0, 0)
                pe.wait_ge(lg_done, 1)
                logits_back(0)

                def body(n, par, first, last):
                    for fb in range(NFB):
                        gate_up(n, par, fb, first)
                        if fb == 0 and first:
                            weights_over(0)
                        if fb == 3 and not first:
                            pe.wait_ge(rwt_done, n + 1)
                            pe.wait_ge(top_done, n + 1)
                            back(n - 1)
                        if fb == 4 and not last:
                            if first:
                                pe.wait_ge(rwt_done, 1)
                                pe.wait_ge(top_done, 1)
                            else:
                                pe.wait_ge(y_added, n * 2)
                            transposes(n + 1, 1 - par)
                        if fb == 6 and not last:
                            router(n + 1, 1 - par)
                        if fb == 7 and not last:
                            pe.wait_ge(lg_done, n + 2)
                        if fb == 9 and not last:
                            weights_over(n + 1)
                        if fb >= 2:
                            down(n, fb - 2)
                        elif not first:
                            down(n - 1, NFB - 2 + fb)
                        if fb == 7 and not last:
                            logits_back(n + 1)

                def tail():
                    down(NCH - 1, NFB - 2)
                    down(NCH - 1, NFB - 1)
                    back(NCH - 1)

                chunks(pe, body, tail)

            @block.scalar
            def _(act):
                def split_w(fb):
                    act.wait_ge(w_in[fb], 16)
                    nc.scalar.copy(w_hi[:, fb, :], w_raw[:, fb % RAW, :]).then_inc(w_hi_done, 1)

                def norm(n):
                    act.wait_ge(rstd_done, n + 1)
                    if not isinstance(n, int) or n > 0:
                        act.wait_ge(xt_ready, n * DB)
                    for j in range(CT):
                        nc.scalar.activation(xn[:, j:j + 1, :], x_sb[:, dyn(n * CT + j), :], ACT.Identity,
                                             bias=nmr[:, j:j + 1], scale=rstd[:, j:j + 1]).then_inc(xn_done, 1)

                def split_xt(n, par):
                    for d in range(DB):
                        act.wait_ge(xt_ready, n * DB + (d + 1))
                        nc.scalar.copy(xt_hi[:, par, d, :], t_ps[d][:]).then_inc(xt_hi_done, 1)

                def logits(n):
                    act.wait_ge(lg_ready, n + 1)
                    if not isinstance(n, int) or n > 0:
                        act.wait_ge(lgt_ready, n)
                    nc.scalar.activation(lg[:], t_ps[0][0:E, :], ACT.Identity, bias=ebias[:, 0:1]).then_inc(lg_done, 1)

                def half_tanh(n):
                    act.wait_ge(gap_done, n + 1)
                    nc.scalar.activation(th[:], gap[:], ACT.Tanh, scale=0.5).then_inc(th_done, 1)

                def weights_out(n):
                    act.wait_ge(rwt_ready, n + 1)
                    if not isinstance(n, int) or n > 0:
                        act.wait_ge(row_done, n * 16)
                    nc.scalar.copy(rwt[:], t_ps[0][0:E, :]).then_inc(rwt_done, 1)

                def silu(n, fb, first):
                    act.wait_ge(g_ready, n * NFB + (fb + 1))
                    if not (first and fb < 2):
                        act.wait_ge(mul_done, n * NFB + (fb - 1))
                    nc.scalar.activation(sil[:, fb % 2, :], g_ps[fb % 2][:], ACT.Silu).then_inc(sil_done, 1)

                def hi(n, fb, first):
                    if fb < NSH:
                        act.wait_ge(mul_done, n * NFB + (fb + 1))
                    else:
                        act.wait_ge(rwmul_done, n * E + (fb - NSH + 1))
                    if not (first and fb < 5):
                        act.wait_ge(down_done, n * NFB + (fb - 4))
                    nc.scalar.copy(h_hi[:, fb % 5, :], hid[:, fb % 2, :]).then_inc(hi_done, 1)

                def out_evac(n):
                    act.wait_ge(down_done, n * NFB + NFB)
                    if not isinstance(n, int) or n > 0:
                        act.wait_ge(back_ready, n * 2)
                    nc.scalar.copy(ot[:, 0, :], o_ps[0][:]).then_inc(ot0_done, 1)

                act.wait_ge(wr_in, 32)
                nc.scalar.copy(wr_hi[:], wr_raw[:]).then_inc(wr_hi_done, 1)
                split_w(0)
                norm(0)
                split_w(1)
                split_xt(0, 0)
                logits(0)
                for fb in range(2, 4):
                    split_w(fb)
                half_tanh(0)
                for fb in range(4, NFB):
                    split_w(fb)
                    if fb == 5:
                        weights_out(0)

                def body(n, par, first, last):
                    for fb in range(NFB):
                        silu(n, fb, first)
                        if fb >= 1:
                            hi(n, fb - 1, first)
                        if fb == 1 and not first:
                            out_evac(n - 1)
                        if not last:
                            if fb == 3:
                                norm(n + 1)
                            if fb == 5:
                                split_xt(n + 1, 1 - par)
                            if fb == 7:
                                logits(n + 1)
                            if fb == 8:
                                half_tanh(n + 1)
                    hi(n, NFB - 1, first)
                    if not last:
                        weights_out(n + 1)

                def tail():
                    out_evac(NCH - 1)

                chunks(act, body, tail)

            @block.vector
            def _(dve):
                def split_w(fb):
                    dve.wait_ge(w_hi_done, fb + 1)
                    nc.vector.tensor_tensor(w_lo[:, fb, :], w_raw[:, fb % RAW, :], w_hi[:, fb, :].bitcast(F32), ALU.subtract).then_inc(w_lo_done, 1)

                def ln_stats(n):
                    if not isinstance(n, int) or n > 0:
                        dve.wait_ge(rstd_done, n)
                    for j in range(CT):
                        ins = nc.vector.bn_stats(stats[:, j, :], x_sb[:, dyn(n * CT + j), :])
                        ins.then_inc(stats_done, 1)
                    wait_apart(nc, dve, c, stats_done, n * CT + CT)
                    for j in range(CT):
                        nc.vector.bn_aggr(mv[:, j, :], stats[:, j, :]).then_inc(mv_done, 1)

                def split_xt(n, par):
                    for d in range(DB):
                        dve.wait_ge(xt_hi_done, n * DB + (d + 1))
                        nc.vector.tensor_tensor(xt_lo[:, par, d, :], t_ps[d][:], xt_hi[:, par, d, :].bitcast(F32), ALU.subtract).then_inc(xt_lo_done, 1)

                STEPS = 14

                def route_top(n):
                    s = n * STEPS
                    wait_apart(nc, dve, c, lgt_ready, n + 1)
                    for j in range(CT):
                        nc.vector.max(top[:, j, :], t_ps[1][:, j * E:(j + 1) * E]).then_inc(dve_step, 1)
                    wait_apart(nc, dve, c, dve_step, s + 4)
                    for j in range(CT):
                        ins = nc.vector.max_index(topi[:, j, :], top[:, j, :], t_ps[1][:, j * E:(j + 1) * E])
                        ins.then_inc(dve_step, 1)
                    nc.vector.tensor_tensor(gap[:], top[:, :, 0], top[:, :, 1], ALU.subtract).then_inc(gap_done, 1)
                    dve.wait_ge(dve_step, s + 8)
                    nc.vector.tensor_copy(topf[:], topi[:, :, 0:2]).then_inc(top_done, 1)
                    dve.wait_ge(top_done, n + 1)
                    for k, hot in ((0, hot1), (1, hot2)):
                        nc.vector.tensor_tensor(hot[:], c.iota8[:].unsqueeze(1).to_broadcast([P, CT, E]),
                                                topf[:, :, k:k + 1].to_broadcast([P, CT, E]), ALU.is_equal).then_inc(dve_step, 1)

                def route_weights(n):
                    s = n * STEPS
                    dve.wait_ge(th_done, n + 1)
                    nc.vector.tensor_scalar(prob[:, :, 0], th[:], 0.5, 0.5, ALU.mult, ALU.add).then_inc(dve_step, 1)
                    nc.vector.tensor_scalar(prob[:, :, 1], th[:], -0.5, 0.5, ALU.mult, ALU.add).then_inc(dve_step, 1)
                    dve.wait_ge(dve_step, s + 12)
                    for k, hot, pr in ((0, hot1, pr1), (1, hot2, pr2)):
                        nc.vector.tensor_tensor(pr[:], hot[:], prob[:, :, k:k + 1].to_broadcast([P, CT, E]), ALU.mult).then_inc(dve_step, 1)
                    dve.wait_ge(dve_step, s + 14)
                    if not isinstance(n, int) or n > 0:
                        dve.wait_ge(rwt_ready, n)
                    nc.vector.tensor_tensor(rw[:], pr1[:], pr2[:], ALU.add).then_inc(rw_done, 1)

                def mul(n, fb, first):
                    k = n * NFB
                    dve.wait_ge(sil_done, k + (fb + 1))
                    dve.wait_ge(u_ready, k + (fb + 1))
                    if fb < NSH:
                        if not first:
                            dve.wait_ge(lo_done, k + (fb - 1))
                        out = hid[:, fb % 2, :]
                    else:
                        if fb >= NSH + 2:
                            dve.wait_ge(rwmul_done, n * E + (fb - NSH - 1))
                        elif not first:
                            dve.wait_ge(rwmul_done, n * E)
                        out = su[:, fb % 2, :]
                    nc.vector.tensor_tensor(out, u_ps[fb % 2][:], sil[:, fb % 2, :], ALU.mult).then_inc(mul_done, 1)

                def lo(n, fb, first):
                    dve.wait_ge(hi_done, n * NFB + (fb + 1))
                    if not (first and fb < 5):
                        dve.wait_ge(down_done, n * NFB + (fb - 4))
                    nc.vector.tensor_tensor(h_lo[:, fb % 5, :], hid[:, fb % 2, :], h_hi[:, fb % 5, :].bitcast(F32), ALU.subtract).then_inc(lo_done, 1)

                def out_evac(n):
                    dve.wait_ge(down_done, n * NFB + NFB)
                    if not isinstance(n, int) or n > 0:
                        dve.wait_ge(back_ready, n * 2)
                    nc.vector.tensor_copy(ot[:, 1, :], o_ps[1][:]).then_inc(ot1_done, 1)

                def add(n):
                    for h in range(2):
                        dve.wait_ge(back_ready, n * 2 + (h + 1))
                        xs = x_sb[:, dyn(n * CT + 2 * h, 2), :]
                        nc.vector.tensor_tensor(xs, t_ps[h][:].rearrange("p (j d) -> p j d", j=2), xs, ALU.add).then_inc(y_added, 1)

                ln_stats(0)
                dve.wait_ge(wr_hi_done, 1)
                nc.vector.tensor_tensor(wr_lo[:], wr_raw[:], wr_hi[:].bitcast(F32), ALU.subtract).then_inc(wr_lo_done, 1)
                split_w(0)
                split_w(1)
                split_xt(0, 0)
                route_top(0)
                for fb in range(2, 4):
                    split_w(fb)
                route_weights(0)
                for fb in range(4, NFB):
                    split_w(fb)

                def body(n, par, first, last):
                    for fb in range(NFB):
                        mul(n, fb, first)
                        if fb >= 1:
                            lo(n, fb - 1, first)
                        if fb == 1 and not first:
                            out_evac(n - 1)
                        if fb == 2 and not last:
                            ln_stats(n + 1)
                        if fb == 4 and not first:
                            add(n - 1)
                        if not last:
                            if fb == 5:
                                split_xt(n + 1, 1 - par)
                            if fb == 8:
                                route_top(n + 1)
                            if fb == 9:
                                route_weights(n + 1)
                    lo(n, NFB - 1, first)

                def tail():
                    out_evac(NCH - 1)
                    add(NCH - 1)

                chunks(dve, body, tail)

            @block.gpsimd
            def _(pool):
                def ln_rstd(n):
                    s = n * 3
                    if not isinstance(n, int) or n > 0:
                        pool.wait_ge(xn_done, n * CT)
                    pool.wait_ge(mv_done, n * CT + CT)
                    nc.gpsimd.tensor_tensor(veps[:], mv[:, :, 1], c.eps[:], ALU.add).then_inc(pool_step, 1)
                    pool.wait_ge(pool_step, s + 1)
                    nc.gpsimd.tensor_tensor(rstd[:], veps[:], c.minus_half[:], ALU.pow).then_inc(pool_step, 1)
                    pool.wait_ge(pool_step, s + 2)
                    nc.gpsimd.tensor_tensor(mr[:], mv[:, :, 0], rstd[:], ALU.mult).then_inc(pool_step, 1)
                    pool.wait_ge(pool_step, s + 3)
                    nc.gpsimd.tensor_tensor(nmr[:], mr[:], c.minus_one[:], ALU.mult).then_inc(rstd_done, 1)

                def broadcast(n):
                    if not isinstance(n, int) or n > 0:
                        pool.wait_ge(rwmul_done, n * E)
                    pool.wait_ge(row_done, n * 16 + 16)
                    nc.gpsimd.tensor_tensor(carrier[:], c.eps[:, 0:1], c.eps[:, 0:1], ALU.add)
                    for e in range(E):
                        nc.gpsimd.partition_broadcast(rw_bc[:, e, :], rw_row[0:1, e, :], P).then_inc(bc_done, 1)

                def weigh(n, fb, first):
                    pool.wait_ge(mul_done, n * NFB + (fb + 1))
                    pool.wait_ge(bc_done, n * E + (fb - NSH + 1))
                    pool.wait_ge(lo_done, n * NFB + (fb - 1))
                    nc.gpsimd.tensor_tensor(hid[:, fb % 2, :], su[:, fb % 2, :], rw_bc[:, fb - NSH, :], ALU.mult).then_inc(rwmul_done, 1)

                ln_rstd(0)
                broadcast(0)

                def body(n, par, first, last):
                    for fb in range(NSH, NFB):
                        weigh(n, fb, first)
                        if fb == 3 and not last:
                            ln_rstd(n + 1)
                    if not last:
                        broadcast(n + 1)

                chunks(pool, body, lambda: None)

        m.clear_sems()


H_A = 16
HD_A = D // H_A
HB_A = P // HD_A
BC = N // CW
BT = N // P
KVW = P + 2 + P
EPS_DEN = 1e-6


def linear_attention_stage(nc, x_sb, c, dram):
    with ExitStack() as ctx:
        m = Mem(nc, ctx, "a")
        w_raw = m.sb("w_raw", [P, DB, 3 * D])
        w_hi = m.sb("w_hi", [P, DB, 3 * D], F32R)
        w_lo = m.sb("w_lo", [P, DB, 3 * D], F32R)
        bq = m.sb("bq", [P, DB])
        bkv_raw = m.sb("bkv_raw", [1, 2 * D])
        bkv = m.sb("bkv", [P, 2 * D], F32R)
        pick = m.sb("pick", [P, P], F32R)
        gamma = m.sb("gamma", [P, D])
        beta = m.sb("beta", [P, D])
        head_mask = m.sb("head_mask", [P, P])
        head_of = m.sb("head_of", [P, HB_A])
        stats = m.sb("stats", [P, CT, 6])
        mv = m.sb("mv", [P, CT, 2])
        veps, rstd, mr, nmr = (m.sb(s, [P, CT]) for s in ("veps", "rstd", "mr", "nmr"))
        xn = m.sb("xn", [P, BT, D])
        xt_hi = m.sb("xt_hi", [P, 2, DB, CW], F32R)
        xt_lo = m.sb("xt_lo", [P, 2, DB, CW], F32R)
        qf = m.sb("qf", [P, 2, CW])
        q_hi = m.sb("q_hi", [P, BC, DB, CW], F32R)
        q_lo = m.sb("q_lo", [P, BC, DB, CW], F32R)
        k_hi = m.sb("k_hi", [P, 2, D], F32R)
        k_lo = m.sb("k_lo", [P, 2, D], F32R)
        v2 = m.sb("v2", [P, 2, DB, KVW], F32R)
        kv_part = m.sb("kv_part", [P, DB, P])
        kv_sum = m.sb("kv_sum", [P, DB, P])
        mix = m.sb("mix", [P, DB, D])
        mix_hi = m.sb("mix_hi", [P, DB, D], F32R)
        mix_lo = m.sb("mix_lo", [P, DB, D], F32R)
        den = m.sb("den", [P, 2, DB, HB_A])
        rden = m.sb("rden", [P, 2, DB, HB_A])
        att = m.sb("att", [P, 2, D])
        y = m.sb("y", [P, CT, D])
        ystats = m.sb("ystats", [P, CT, 6])
        ymv = m.sb("ymv", [P, CT, 2])
        yveps, yrstd, ymr, ynmr = (m.sb(s, [P, CT]) for s in ("yveps", "yrstd", "ymr", "ynmr"))
        yn = m.sb("yn", [P, CT, D])
        yg = m.sb("yg", [P, CT, D])
        yb = m.sb("yb", [P, CT, D])
        t_ps = [m.ps(f"t{i}", [P, CW]) for i in range(2)]
        p_ps = [m.ps(f"p{i}", [P, 2 * D]) for i in range(2)]
        kv_ps = [m.ps(f"kv{i}", [P, 2 * D]) for i in range(DB)]
        cx_ps = [m.ps(f"cx{i}", [P, DB, D]) for i in range(2)]

        w_in, small_in = m.sem("w_in"), m.sem("small_in")
        w_hi_done, w_lo_done, zeroed, set_up = m.sem("w_hi_done"), m.sem("w_lo_done"), m.sem("zeroed"), m.sem("set_up")
        stats_done, mv_done, pool_step = m.sem("stats_done"), m.sem("mv_done"), m.sem("pool_step")
        rstd_done, xn_done = m.sem("rstd_done"), m.sem("xn_done")
        xt_ready, xt_hi_done, xt_lo_done = m.sem("xt_ready"), m.sem("xt_hi_done"), m.sem("xt_lo_done")
        q_ready, qf_done, q_hi_done, q_lo_done = m.sem("q_ready"), m.sem("qf_done"), m.sem("q_hi_done"), m.sem("q_lo_done")
        p_ready, kv_hi_done, kv_lo_done, kvacc_done = m.sem("p_ready"), m.sem("kv_hi_done"), m.sem("kv_lo_done"), m.sem("kvacc_done")
        part_done, mix_step, mix_hi_done, mix_lo_done = m.sem("part_done"), m.sem("mix_step"), m.sem("mix_hi_done"), m.sem("mix_lo_done")
        cx_ready, out_step, att_done, y_done = m.sem("cx_ready"), m.sem("out_step"), m.sem("att_done"), m.sem("y_done")
        ystats_done, ymv_done, ypool_step, yrstd_done = m.sem("ystats_done"), m.sem("ymv_done"), m.sem("ypool_step"), m.sem("yrstd_done")
        yn_done, yg_done, yb_done, x_added = m.sem("yn_done"), m.sem("yg_done"), m.sem("yb_done"), m.sem("x_added")

        def sequences(eng, body):
            body(0, True, False)
            with loop(nc, eng, 1, B - 1) as b:
                body(b, False, False)
            body(B - 1, False, True)

        with nc.Block() as block:

            @block.sync
            def _(sp):
                sp.dma_start(w_raw[:], dram["w_qkv_a"]).then_inc(w_in, 16)
                sp.dma_start(bkv_raw[:], dram["b_kv_a"]).then_inc(w_in, 16)
                for tile, name in ((bq, "b_q_a"), (head_mask, "head_mask"), (head_of, "head_of")):
                    sp.dma_start(tile[:], dram[name]).then_inc(small_in, 16)
                for tile, name in ((gamma, "gamma"), (beta, "beta")):
                    sp.dma_start(tile[:], dram[name].to_broadcast([P, D])).then_inc(small_in, 16)

            @block.tensor
            def _(pe):
                def transposes(n, c_, fresh):
                    pe.wait_ge(xn_done, n * CT + CT)
                    if not fresh:
                        pe.wait_ge(qf_done, n * DB)
                    for d in range(DB):
                        for j in range(CT):
                            last = nc.tensor.transpose(t_ps[d][:, j * P:(j + 1) * P], xn[:, c_ * CT + j, d * P:(d + 1) * P], c.ident[:])
                        last.then_inc(xt_ready, 1)

                def queries(n, c_):
                    pe.wait_ge(xt_hi_done, n * DB + DB)
                    pe.wait_ge(xt_lo_done, n * DB + DB)
                    for o in range(DB):
                        k = 0
                        for d in range(DB):
                            for w, xt in ((w_hi, xt_hi), (w_hi, xt_lo), (w_lo, xt_hi)):
                                last = nc.tensor.matmul(t_ps[o][:], w[:, d, o * P:(o + 1) * P], xt[:, c_, d, :], start=(k == 0), stop=(k == 5))
                                k += 1
                        last.then_inc(q_ready, 1)

                def keys_values(t, i, fresh):
                    if not fresh:
                        pe.wait_ge(kv_lo_done, (t - 1) * 2)
                    ps = p_ps[i % 2]
                    nc.tensor.matmul(ps[:], pick[:], bkv[:], start=True, stop=False)
                    cols = slice((i % CT) * P, (i % CT + 1) * P)
                    for d in range(DB):
                        for xt, w in ((xt_hi, w_hi), (xt_hi, w_lo), (xt_lo, w_hi)):
                            last = nc.tensor.matmul(ps[:], xt[:, i // CT, d, cols], w[:, d, D:], start=False, stop=(d == 1 and xt is xt_lo))
                    last.then_inc(p_ready, 1)

                def accumulate(t, i):
                    pe.wait_ge(kv_lo_done, t * 2 + 2)
                    for j in range(DB):
                        for k in (k_hi, k_lo):
                            last = nc.tensor.matmul(kv_ps[j][:, 0:KVW], k[:, i % 2, j * P:(j + 1) * P], v2[:, i % 2, j, :],
                                                    start=(i == 0 and k is k_hi), stop=(i == BT - 1 and k is k_lo))
                    last.then_inc(kvacc_done, 1)

                def context(t, i, fresh):
                    if not fresh:
                        pe.wait_ge(att_done, t - 1)
                    cols = slice((i % CT) * P, (i % CT + 1) * P)
                    for j in range(DB):
                        for k, (q, w) in enumerate(((q_hi, mix_hi), (q_hi, mix_lo), (q_lo, mix_hi))):
                            last = nc.tensor.matmul(cx_ps[i % 2][:, j, :], q[:, i // CT, j, cols], w[:, j, :], start=(k == 0), stop=(k == 2))
                    last.then_inc(cx_ready, 1)

                pe.wait_ge(set_up, 2)
                pe.wait_ge(w_lo_done, 2)

                def body(b, first, last):
                    n, t = b * BC, b * BT
                    transposes(n, 0, first)
                    queries(n, 0)
                    for i in range(BT):
                        keys_values(t + i, i, first and i < 2)
                        if i >= 1:
                            accumulate(t + (i - 1), i - 1)
                        if i == 1:
                            transposes(n + 1, 1, False)
                        if i == CT - 1:
                            queries(n + 1, 1)
                    accumulate(t + (BT - 1), BT - 1)
                    pe.wait_ge(mix_hi_done, b + 1)
                    pe.wait_ge(mix_lo_done, b + 1)
                    pe.wait_ge(q_hi_done, n * DB + 2 * DB)
                    pe.wait_ge(q_lo_done, n * DB + 2 * DB)
                    for i in range(BT):
                        context(t + i, i, first and i < 2)

                sequences(pe, body)

            @block.scalar
            def _(act):
                def norm(n, c_, fresh):
                    act.wait_ge(rstd_done, n + 1)
                    if not fresh:
                        act.wait_ge(y_done, (n - 1) * CT)
                    for j in range(CT):
                        nc.scalar.activation(xn[:, c_ * CT + j:c_ * CT + j + 1, :], x_sb[:, dyn(n * CT + j), :], ACT.Identity,
                                             bias=nmr[:, j:j + 1], scale=rstd[:, j:j + 1]).then_inc(xn_done, 1)

                def split_xt(n, c_):
                    for d in range(DB):
                        act.wait_ge(xt_ready, n * DB + (d + 1))
                        nc.scalar.copy(xt_hi[:, c_, d, :], t_ps[d][:]).then_inc(xt_hi_done, 1)

                def split_q(n, c_):
                    for o in range(DB):
                        act.wait_ge(qf_done, n * DB + (o + 1))
                        nc.scalar.copy(q_hi[:, c_, o, :], qf[:, o, :]).then_inc(q_hi_done, 1)

                def split_kv(t, i, fresh):
                    act.wait_ge(p_ready, t + 1)
                    if not fresh:
                        act.wait_ge(kvacc_done, t - 1)
                    ps = p_ps[i % 2]
                    nc.scalar.activation(k_hi[:, i % 2, :], ps[:, 0:D], ACT.Relu).then_inc(kv_hi_done, 1)
                    nc.scalar.copy(v2[:, i % 2, :, 0:P], ps[:, D:].rearrange("p (j v) -> p j v", j=DB)).then_inc(kv_hi_done, 1)

                act.wait_ge(w_in, 32)
                nc.scalar.copy(w_hi[:], w_raw[:]).then_inc(w_hi_done, 1)
                act.wait_ge(zeroed, 3)
                nc.scalar.copy(bkv[0:1, :], bkv_raw[:]).then_inc(w_hi_done, 1)
                norm(0, 0, True)

                def body(b, first, last):
                    n, t = b * BC, b * BT
                    split_xt(n, 0)
                    norm(n + 1, 1, first)
                    split_q(n, 0)
                    for i in range(BT):
                        split_kv(t + i, i, first and i < 2)
                        if i == 1:
                            split_xt(n + 1, 1)
                        if i == CT - 1:
                            split_q(n + 1, 1)
                    act.wait_ge(kvacc_done, t + BT)
                    for j in range(DB):
                        nc.scalar.copy(kv_part[:, j, :], kv_ps[j][:, P + 2:KVW]).then_inc(part_done, 1)
                    act.wait_ge(mix_step, b * 6 + 6)
                    nc.scalar.copy(mix_hi[:], mix[:]).then_inc(mix_hi_done, 1)
                    for h in range(BC):
                        act.wait_ge(yrstd_done, n + (h + 1))
                        if not (first and h == 0):
                            act.wait_ge(yg_done, (n + h) * CT)
                        for j in range(CT):
                            nc.scalar.activation(yn[:, j, :], y[:, j, :], ACT.Identity, bias=ynmr[:, j:j + 1],
                                                 scale=yrstd[:, j:j + 1]).then_inc(yn_done, 1)
                        if h == 0 and not last:
                            norm(n + BC, 0, False)

                sequences(act, body)

            @block.vector
            def _(dve):
                def ln_stats(n, fresh):
                    if not fresh:
                        dve.wait_ge(rstd_done, n)
                    for j in range(CT):
                        nc.vector.bn_stats(stats[:, j, :], x_sb[:, dyn(n * CT + j), :]).then_inc(stats_done, 1)
                    wait_apart(nc, dve, c, stats_done, n * CT + CT)
                    for j in range(CT):
                        nc.vector.bn_aggr(mv[:, j, :], stats[:, j, :]).then_inc(mv_done, 1)

                def split_xt(n, c_):
                    for d in range(DB):
                        dve.wait_ge(xt_hi_done, n * DB + (d + 1))
                        nc.vector.tensor_tensor(xt_lo[:, c_, d, :], t_ps[d][:], xt_hi[:, c_, d, :].bitcast(F32), ALU.subtract).then_inc(xt_lo_done, 1)

                def relu_q(n, fresh):
                    for o in range(DB):
                        dve.wait_ge(q_ready, n * DB + (o + 1))
                        if not fresh:
                            dve.wait_ge(q_hi_done, (n - 1) * DB + (o + 1))
                            dve.wait_ge(q_lo_done, (n - 1) * DB + (o + 1))
                        nc.vector.tensor_scalar(qf[:, o, :], t_ps[o][:], bq[:, o:o + 1], 0.0, ALU.add, ALU.max).then_inc(qf_done, 1)

                def split_kv(t, i):
                    ps = p_ps[i % 2]
                    dve.wait_ge(kv_hi_done, t * 2 + 2)
                    nc.vector.scalar_tensor_tensor(out=k_lo[:, i % 2, :], in0=ps[:, 0:D], scalar=0.0, in1=k_hi[:, i % 2, :].bitcast(F32),
                                                   op0=ALU.max, op1=ALU.subtract).then_inc(kv_lo_done, 1)
                    nc.vector.tensor_tensor(v2[:, i % 2, :, P + 2:], ps[:, D:].rearrange("p (j v) -> p j v", j=DB),
                                            v2[:, i % 2, :, 0:P].bitcast(F32), ALU.subtract).then_inc(kv_lo_done, 1)

                nc.vector.memset(bkv[:].bitcast(F32), 0.0).then_inc(zeroed, 1)
                nc.vector.memset(pick[:].bitcast(F32), 0.0).then_inc(zeroed, 1)
                nc.vector.memset(mix[:], 0.0).then_inc(zeroed, 1)
                nc.vector.memset(v2[:, :, :, P:P + 2].bitcast(F32), 1.0).then_inc(set_up, 1)
                ln_stats(0, True)
                dve.wait_ge(zeroed, 3)
                for r in (0, 32):
                    last = nc.vector.memset(pick[r:r + 1, :].bitcast(F32), 1.0)
                last.then_inc(set_up, 1)
                dve.wait_ge(w_hi_done, 1)
                nc.vector.tensor_tensor(w_lo[:], w_raw[:], w_hi[:].bitcast(F32), ALU.subtract).then_inc(w_lo_done, 1)
                dve.wait_ge(w_hi_done, 2)
                nc.vector.tensor_tensor(bkv[32:33, :], bkv_raw[:], bkv[0:1, :].bitcast(F32), ALU.subtract).then_inc(w_lo_done, 1)
                dve.wait_ge(small_in, 16 * 5)

                def body(b, first, last):
                    n, t = b * BC, b * BT
                    split_xt(n, 0)
                    ln_stats(n + 1, False)
                    relu_q(n, first)
                    for i in range(BT):
                        split_kv(t + i, i)
                        if i == 1:
                            split_xt(n + 1, 1)
                        if i == CT - 1:
                            relu_q(n + 1, False)
                    if not last:
                        ln_stats(n + BC, False)
                    dve.wait_ge(kvacc_done, t + BT)
                    if not first:
                        dve.wait_ge(mix_lo_done, b)
                    for j in range(DB):
                        dve.wait_ge(part_done, b * DB + (j + 1))
                        nc.vector.tensor_tensor(kv_sum[:, j, :], kv_ps[j][:, 0:P], kv_part[:, j, :], ALU.add).then_inc(mix_step, 1)
                        nc.vector.tensor_scalar(mix[:, j, P:P + HB_A], head_of[:], kv_ps[j][:, P:P + 1], None, ALU.mult).then_inc(mix_step, 1)
                    dve.wait_ge(mix_step, b * 6 + 4)
                    for j in range(DB):
                        nc.vector.tensor_tensor(mix[:, j, 0:P], kv_sum[:, j, :], head_mask[:], ALU.mult).then_inc(mix_step, 1)
                    dve.wait_ge(mix_hi_done, b + 1)
                    nc.vector.tensor_tensor(mix_lo[:], mix[:], mix_hi[:].bitcast(F32), ALU.subtract).then_inc(mix_lo_done, 1)
                    for h in range(BC):
                        for g in range(CT // 2):
                            i = h * CT + g * 2
                            s = (t + i) // 2 if isinstance(t, int) else b * (BT // 2) + i // 2
                            for k in range(2):
                                dve.wait_ge(cx_ready, t + (i + k + 1))
                                nc.vector.tensor_scalar(den[:, k], cx_ps[k][:, :, P:P + HB_A], EPS_DEN, None, ALU.max).then_inc(out_step, 1)
                            dve.wait_ge(out_step, s * 3 + 2)
                            nc.vector.reciprocal(rden[:], den[:]).then_inc(out_step, 1)
                            dve.wait_ge(out_step, s * 3 + 3)
                            for k in range(2):
                                nc.vector.tensor_tensor(att[:, k, :].rearrange("p (j h e) -> p j h e", j=DB, h=HB_A),
                                                        cx_ps[k][:, :, 0:P].rearrange("p j (h e) -> p j h e", h=HB_A),
                                                        rden[:, k].unsqueeze(3).to_broadcast([P, DB, HB_A, HD_A]), ALU.mult).then_inc(att_done, 1)
                            dve.wait_ge(att_done, t + (i + 2))
                            if g == 0 and not (first and h == 0):
                                dve.wait_ge(yn_done, (n + h) * CT)
                            for k in range(2):
                                j = g * 2 + k
                                nc.vector.tensor_tensor(y[:, j, :], att[:, k, :], xn[:, i + k, :], ALU.add).then_inc(y_done, 1)
                            dve.wait_ge(y_done, t + (i + 2))
                            for k in range(2):
                                j = g * 2 + k
                                nc.vector.bn_stats(ystats[:, j, :], y[:, j, :]).then_inc(ystats_done, 1)
                        wait_apart(nc, dve, c, ystats_done, t + (h * CT + CT))
                        for j in range(CT):
                            nc.vector.bn_aggr(ymv[:, j, :], ystats[:, j, :]).then_inc(ymv_done, 1)

                sequences(dve, body)

            @block.gpsimd
            def _(pool):
                def rstd_of(n, mv, veps, rstd, mr, nmr, ready, step, done, read, fresh):
                    if not fresh:
                        pool.wait_ge(read, n * CT)
                    pool.wait_ge(ready, n * CT + CT)
                    nc.gpsimd.tensor_tensor(veps[:], mv[:, :, 1], c.eps[:], ALU.add).then_inc(step, 1)
                    pool.wait_ge(step, n * 3 + 1)
                    nc.gpsimd.tensor_tensor(rstd[:], veps[:], c.minus_half[:], ALU.pow).then_inc(step, 1)
                    pool.wait_ge(step, n * 3 + 2)
                    nc.gpsimd.tensor_tensor(mr[:], mv[:, :, 0], rstd[:], ALU.mult).then_inc(step, 1)
                    pool.wait_ge(step, n * 3 + 3)
                    nc.gpsimd.tensor_tensor(nmr[:], mr[:], c.minus_one[:], ALU.mult).then_inc(done, 1)

                def ln_rstd(n, fresh):
                    rstd_of(n, mv, veps, rstd, mr, nmr, mv_done, pool_step, rstd_done, xn_done, fresh)

                def split_q(n, c_):
                    for o in range(DB):
                        pool.wait_ge(q_hi_done, n * DB + (o + 1))
                        nc.gpsimd.tensor_tensor(q_lo[:, c_, o, :], qf[:, o, :], q_hi[:, c_, o, :].bitcast(F32), ALU.subtract).then_inc(q_lo_done, 1)

                ln_rstd(0, True)
                pool.wait_ge(small_in, 16 * 5)

                def body(b, first, last):
                    n = b * BC
                    ln_rstd(n + 1, False)
                    split_q(n, 0)
                    split_q(n + 1, 1)
                    if not last:
                        ln_rstd(n + BC, False)
                    for h in range(BC):
                        rstd_of(n + h, ymv, yveps, yrstd, ymr, ynmr, ymv_done, ypool_step, yrstd_done, yn_done, first and h == 0)
                        u = (n + h) * CT
                        for j in range(CT):
                            pool.wait_ge(yn_done, u + (j + 1))
                            nc.gpsimd.tensor_tensor(yg[:, j, :], yn[:, j, :], gamma[:], ALU.mult).then_inc(yg_done, 1)
                        for j in range(CT):
                            pool.wait_ge(yg_done, u + (j + 1))
                            nc.gpsimd.tensor_tensor(yb[:, j, :], yg[:, j, :], beta[:], ALU.add).then_inc(yb_done, 1)
                        for j in range(CT):
                            pool.wait_ge(yb_done, u + (j + 1))
                            xs = x_sb[:, dyn(u + j), :]
                            nc.gpsimd.tensor_tensor(xs, xs, yb[:, j:j + 1, :], ALU.add).then_inc(x_added, 1)

                sequences(pool, body)

        m.clear_sems()


H_B, HD_B = 8, 64
INNER = H_B * HD_B
NPAIR = H_B // 2
NU = BT // 2
UNITS = H_B * NU
BUCKETS, MAX_DIST = 32, 128
NEAR = 2 * P
SPAN = 3 * P
MASKED = -1e30
SCALE_B = HD_B ** -0.5
LOWEST = -3e38


def softmax_attention_stage(nc, x_sb, c, dram):
    with ExitStack() as ctx:
        m = Mem(nc, ctx, "b")
        prob = m.sb("prob", [P, 2, 2, N])
        w_raw = prob[:].rearrange("p a t k -> p (a t k)")
        WQKV = DB * 3 * INNER
        w_hi = m.sb("w_hi", [P, DB, 3 * INNER], F32R)
        w_lo = m.sb("w_lo", [P, DB, 3 * INNER], F32R)
        wo_hi = m.sb("wo_hi", [P, NPAIR, D], F32R)
        wo_lo = m.sb("wo_lo", [P, NPAIR, D], F32R)
        bo_raw = m.sb("bo_raw", [1, 2 * D])
        bo = m.sb("bo", [P, 2 * D], F32R)
        pick = m.sb("pick", [P, P], F32R)
        rel = m.sb("rel", [BUCKETS + 1, H_B])
        by_dist = m.sb("by_dist", [BUCKETS + 1, SPAN])
        bias = m.sb("bias", [P, H_B, NEAR])
        zeros = m.sb("zeros", [P, P])
        stats = m.sb("stats", [P, CT, 6])
        mv = m.sb("mv", [P, CT, 2])
        veps, rstd, mr, nmr = (m.sb(s, [P, CT]) for s in ("veps", "rstd", "mr", "nmr"))
        xn = m.sb("xn", [P, CT, D])
        xt_hi = m.sb("xt_hi", [P, BC, DB, CW], F32R)
        xt_lo = m.sb("xt_lo", [P, BC, DB, CW], F32R)
        q2 = m.sb("q2", [P, 2, 2, N], F32R)
        kn_hi = m.sb("kn_hi", [P, N], F32R)
        kn_lo = m.sb("kn_lo", [P, N], F32R)
        k_hi2 = m.sb("k_hi2", [P, 2, N], F32R)
        k_lo2 = m.sb("k_lo2", [P, 2, N], F32R)
        v2 = m.sb("v2", [P, BT, 4, 2 * HD_B], F32R)
        mx = m.sb("mx", [P, 2, 2])
        nmx = m.sb("nmx", [P, 2, 2])
        psum_of = m.sb("psum_of", [P, 2, 2])
        rsum = m.sb("rsum", [P, 2, 2])
        pt_hi = m.sb("pt_hi", [P, BT, 2 * P], F32R)
        pt_lo = m.sb("pt_lo", [P, BT, 2 * P], F32R)
        oa = m.sb("oa", [P, NU, 2 * P])
        ob = m.sb("ob", [P, NU, 2 * P])
        osum = m.sb("osum", [P, 2 * P])
        band_last = m.sb("band_last", [P, SPAN])
        band = [part[:].rearrange("p a b -> p (a b)")[:, i * SPAN:(i + 1) * SPAN] for part, n in ((bias, 5), (ob, 2)) for i in range(n)] + [band_last[:]]
        rel_wide = oa[0:BUCKETS + 1].rearrange("p u q -> p (u q)").rearrange("p (h q) -> p h q", h=H_B)
        o_hi = m.sb("o_hi", [P, N], F32R)
        o_lo = m.sb("o_lo", [P, N], F32R)
        norm_carrier, sum_carrier = m.sb("norm_carrier", [P, 1]), m.sb("sum_carrier", [P, 1])
        band_dram = nc.dram_tensor("band_scratch", (H_B, P, SPAN), F32, kind="Internal").ap()
        s_ps = [m.ps(f"s{i}", [P, N]) for i in range(2)]
        pt_ps = [m.ps(f"pt{i}", [P, 2, 2 * P]) for i in range(2)]
        o_ps = m.ps("o", [P, 2 * P * 2])
        j_ps = m.ps("j", [P, CW])

        w_in, small_in, zeroed, set_up = m.sem("w_in"), m.sem("small_in"), m.sem("zeroed"), m.sem("set_up")
        w_hi_done, w_lo_done = m.sem("w_hi_done"), m.sem("w_lo_done")
        rel_done, band_ready, band_done, band_out, bias_in = (m.sem(s) for s in ("rel_done", "band_ready", "band_done", "band_out", "bias_in"))
        stats_done, mv_done, pool_step, rstd_done, xn_done = (m.sem(s) for s in ("stats_done", "mv_done", "pool_step", "rstd_done", "xn_done"))
        j_ready, job_hi, j_done = m.sem("j_ready"), m.sem("job_hi"), m.sem("j_done")
        k_in = [m.sem(f"k_in{s}") for s in range(2)]
        s_ready, mx_step, nmx_done, exp_done, rsum_done, norm_done = (m.sem(s) for s in ("s_ready", "mx_step", "nmx_done", "exp_done", "rsum_done", "norm_done"))
        pt_ready, pt_hi_done, pt_lo_done, pv_done = (m.sem(s) for s in ("pt_ready", "pt_hi_done", "pt_lo_done", "pv_done"))
        o_out, o_step, o_done = m.sem("o_out"), m.sem("o_step"), m.sem("o_done")

        TRI = [u * (u + 1) // 2 for u in range(NU + 1)]
        BANKS = H_B * TRI[NU]

        def unit(k):
            return k // NU, k % NU

        def banks_before(b, k):
            return b * BANKS + ((k // NU) * TRI[NU] + TRI[k % NU])

        def bank_of(k, i):
            h, u = unit(k)
            return pt_ps[(h * TRI[NU] + TRI[u] + i) % 2]

        def jobs_at(k, first, last):
            p, r = k // (2 * NU), k % (2 * NU)
            out = []
            if p % 2 == 0 and 1 <= r <= NU:
                out.append(("v", p // 2, r - 1))
            if r <= 2 and not (first and p == 0):
                out.append(("y", p - 1, r + 1))
            if r == 7:
                out.append(("y", p, 0))
            if not (last and p == NPAIR - 1):
                if p == NPAIR - 1 and r < BC:
                    out += [("x", r, d) for d in range(DB)]
                if r in (3, 4):
                    out.append(("k", p + 1, r - 3))
                if r in (5, 6):
                    out.append(("q", p + 1, r - 5))
            return out

        def splits(jobs):
            return sum(j[0] != "y" for j in jobs)

        PRO = [("x", n, d) for n in range(BC) for d in range(DB)] + [(kind, NPAIR, n) for kind in "kq" for n in range(BC)]
        JOBS = [sum((jobs_at(k, f, False) for k in range(UNITS)), []) for f in (True, False)]

        def plan(b, first, last):
            at = len(PRO) if first else b * len(JOBS[1]) + (len(PRO) + len(JOBS[0]) - len(JOBS[1]))
            split_at = b * splits(JOBS[1]) + len(PRO)
            steps, n, ns = [], 0, 0
            number = {("y", -2, u): at + (JOBS[1].index(("y", NPAIR - 2, u)) - len(JOBS[1])) for u in range(NU) if not first}
            for k in range(UNITS):
                steps.append([])
                for j in jobs_at(k, first, last):
                    number[j] = at + n
                    steps[-1].append((j, at + n, split_at + ns))
                    n, ns = n + 1, ns + (j[0] != "y")
            return steps, number

        LAST, LAST_NUMBER = plan(B - 1, False, True)
        TAIL_AT = (B - 1) * len(JOBS[1]) + (len(PRO) + len(JOBS[0]) - len(JOBS[1])) + sum(len(s) for s in LAST)
        TAIL = [(("y", NPAIR - 1, u), TAIL_AT + u - 1) for u in range(1, NU)]

        def sequences(eng, body):
            body(0, True, False)
            with loop(nc, eng, 1, B - 1) as b:
                body(b, False, False)
            body(B - 1, False, True)

        def after(b, k):
            return (b, k + 1) if k < UNITS - 1 else (b + 1, 0)

        def before(b, k):
            return (b, k - 1) if k else (b - 1, UNITS - 1)

        with nc.Block() as block:

            @block.sync
            def _(sp):
                sp.dma_start(w_raw[:, :WQKV], dram["w_qkv_b"]).then_inc(w_in, 16)
                sp.dma_start(w_raw[:, WQKV:], dram["w_o_b"]).then_inc(w_in, 16)
                for tile, name in ((bo_raw, "b_o_b"), (rel, "rel_emb"), (by_dist, "by_dist")):
                    sp.dma_start(tile[:], dram[name]).then_inc(small_in, 16)
                for h in range(H_B):
                    sp.wait_ge(band_done, h + 1)
                    sp.dma_start(band_dram[h], band[h]).then_inc(band_out, 16)
                sp.wait_ge(band_out, 16 * H_B)
                for h in range(H_B):
                    skewed = bass.AP(tensor=band_dram.tensor, offset=h * P * SPAN + P - 1, ap=[[SPAN - 1, P], [1, NEAR]])
                    sp.dma_start(bias[:, h, :], skewed).then_inc(bias_in, 16)

                def spread(g, number, fresh):
                    sp.wait_ge(j_done, number + 1)
                    for s in range(2):
                        if not fresh:
                            sp.wait_ge(s_ready, g * (4 * NU) + 2 * NU * (s - 1))
                        rows = slice(s * HD_B, (s + 1) * HD_B)
                        for dst, src in ((k_hi2, kn_hi), (k_lo2, kn_lo)):
                            for half in range(2):
                                sp.dma_start(dst[half * HD_B:(half + 1) * HD_B, s, :].bitcast(F32), src[rows, :].bitcast(F32)).then_inc(k_in[s], 16)

                spread(0, PRO.index(("k", NPAIR, BC - 1)), True)

                def body(b, first, last):
                    _, number = plan(b, first, last)
                    for p in range(1, NPAIR + (not last)):
                        spread(b * NPAIR + p, number["k", p, BC - 1], False)

                sequences(sp, body)

            @block.tensor
            def _(pe):
                three = lambda x, y: ((x[0], y[0]), (x[0], y[1]), (x[1], y[0]))
                xt, w = (xt_hi, xt_lo), (w_hi, w_lo)

                def scores(b, k, t, q_number, fresh):
                    K = b * UNITS + k
                    h, u = unit(k)
                    s = h % 2
                    if u == 0 and t == 0:
                        if s == 0:
                            pe.wait_ge(j_done, q_number + 1)
                        pe.wait_ge(k_in[s], (b * NPAIR + h // 2) * 64 + 64)
                    if not fresh:
                        pe.wait_ge(exp_done, K * 2 + (t - 1))
                    cols = slice((2 * u + t) * P, (2 * u + t + 1) * P)
                    width = 2 * P * (u + 1)
                    for lo in range(0, width, CW):
                        hi = min(width, lo + CW)
                        for kk in (k_hi2, k_lo2):
                            last = nc.tensor.matmul(s_ps[t][:, lo:hi], q2[:, (h // 2) % 2, s, cols], kk[:, s, lo:hi], start=kk is k_hi2, stop=kk is k_lo2)
                    last.then_inc(s_ready, 1)

                def turn(b, k, i, fresh):
                    u = unit(k)[1]
                    nb = banks_before(b, k) + i
                    if i == 0:
                        pe.wait_ge(norm_done, (b * UNITS + k) * 2 + 2)
                    if not fresh:
                        pe.wait_ge(pt_lo_done, nb - 1)
                    bank = bank_of(k, i)
                    for a in range(2):
                        kt = 2 * i + a
                        for t in range(2):
                            src = zeros[:] if kt > 2 * u + t else prob[:, k % 2, t, kt * P:(kt + 1) * P]
                            last = nc.tensor.transpose(bank[:, a, t * P:(t + 1) * P], src, c.ident[:])
                    last.then_inc(pt_ready, 1)

                def product(b, k, i, v_number, fresh):
                    u = unit(k)[1]
                    pe.wait_ge(pt_lo_done, banks_before(b, k) + (i + 1))
                    if i == 0 and not fresh:
                        pe.wait_ge(o_out, (b * UNITS + k) * 2)
                    if v_number is not None:
                        pe.wait_ge(j_done, v_number + 1)
                    for a in range(2):
                        kt = 2 * i + a
                        for pt in (pt_hi, pt_lo):
                            last = nc.tensor.matmul(o_ps[:, 0:2 * P], v2[:, kt, unit(k)[0] % 4, :], pt[:, kt, :],
                                                    start=(kt == 0 and pt is pt_hi), stop=(kt == 2 * u + 1 and pt is pt_lo))
                    if i == u:
                        last.then_inc(pv_done, 1)

                def job(b, j, number):
                    kind, a, i = j
                    if not (isinstance(number, int) and number == 0):
                        pe.wait_ge(j_done, number)
                    if kind == "x":
                        pe.wait_ge(xn_done, (b + 1) * (BC * CT) + (a + 1) * CT)
                        for t in range(CT):
                            last = nc.tensor.transpose(j_ps[:, t * P:(t + 1) * P], xn[:, t, i * P:(i + 1) * P], c.ident[:])
                    if kind in "kq":
                        lo = (INNER if kind == "k" else 0) + (a % NPAIR) * P
                        terms = [(ww[:, d, lo:lo + P], xx[:, i, d, :]) for d in range(DB) for ww, xx in three(w, xt)]
                        for n, (ww, xx) in enumerate(terms):
                            last = nc.tensor.matmul(j_ps[:], ww, xx, start=(n == 0), stop=(n == len(terms) - 1))
                    if kind == "v":
                        lo = 2 * INNER + a * D
                        for t in range(2):
                            kt = 2 * i + t
                            cols = slice((kt % CT) * P, (kt % CT + 1) * P)
                            terms = [(xx[:, kt // CT, d, cols], ww[:, d, lo:lo + D]) for d in range(DB) for xx, ww in three(xt, w)]
                            for n, (xx, ww) in enumerate(terms):
                                last = nc.tensor.matmul(j_ps[:, t * D:(t + 1) * D], xx, ww, start=(n == 0), stop=(n == len(terms) - 1))
                    if kind == "y":
                        pe.wait_ge(o_done, (b * NPAIR + a) * NU + (i + 1))
                        pair = a % NPAIR
                        if pair == 0:
                            nc.tensor.matmul(j_ps[:], pick[:], bo[:], start=True, stop=False)
                        for t in range(2):
                            cols = slice((2 * i + t) * P, (2 * i + t + 1) * P)
                            for n, (oo, ww) in enumerate(three((o_hi, o_lo), (wo_hi, wo_lo))):
                                last = nc.tensor.matmul(j_ps[:, t * D:(t + 1) * D], oo[:, cols], ww[:, pair, :],
                                                        start=(n == 0 and pair > 0), stop=(n == 2 and (pair > 0 or t == 1)))
                    last.then_inc(j_ready, 1)

                pe.wait_ge(rel_done, 1)
                pe.wait_ge(small_in, 48)
                for h in range(H_B):
                    if h >= 4:
                        pe.wait_ge(band_done, h - 3)
                    lo = (h // 2 % 2) * CW
                    nc.tensor.matmul(s_ps[h % 2][:, lo:lo + SPAN], rel_wide[:, h, :], by_dist[:], start=True, stop=True).then_inc(band_ready, 1)
                pe.wait_ge(w_lo_done, 3)
                pe.wait_ge(set_up, 2)
                for i, j in enumerate(PRO):
                    job(-1, j, i)
                pe.wait_ge(band_done, H_B)
                for t in range(2):
                    scores(0, 0, t, len(PRO) - 1, True)

                def body(b, first, last):
                    steps, number = plan(b, first, last)
                    for k in range(UNITS):
                        jobs = list(steps[k])
                        for t in range(2):
                            if not (last and k == UNITS - 1):
                                scores(*after(b, k), t, number.get(("q", (k + 1) // (2 * NU), BC - 1)), False)
                            if t == 0 and jobs:
                                job(b, *jobs.pop(0)[:2])
                        u = unit(k)[1]
                        pb, pk = before(b, k)
                        ph, pu = unit(pk)
                        if first and k == 0:
                            pu = -1
                        for i in range(max(u, pu) + 1):
                            if i <= pu:
                                product(pb, pk, i, number["v", ph // 4, i] if ph % 4 == 0 and i == pu else None, first and k == 1)
                            if i <= u:
                                turn(b, k, i, first and banks_before(0, k) + i < 2)
                            if jobs:
                                job(b, *jobs.pop(0)[:2])
                        while jobs:
                            job(b, *jobs.pop(0)[:2])

                sequences(pe, body)
                for i in range(NU):
                    product(B - 1, UNITS - 1, i, None, False)
                for j, number in TAIL:
                    job(B - 1, j, number)

            @block.scalar
            def _(act):
                def norm(n):
                    act.wait_ge(rstd_done, n + 1)
                    for j in range(CT):
                        nc.scalar.activation(xn[:, j:j + 1, :], x_sb[:, dyn(n * CT + j), :], ACT.Identity,
                                             bias=nmr[:, j:j + 1], scale=rstd[:, j:j + 1]).then_inc(xn_done, 1)

                def job(b, j, number, fresh=False):
                    kind, a, i = j
                    if kind == "y":
                        return
                    act.wait_ge(j_ready, number + 1)
                    cols = slice(i * CW, (i + 1) * CW)
                    if kind == "x":
                        last = nc.scalar.copy(xt_hi[:, a, i, :], j_ps[:])
                    if kind == "k":
                        if not fresh:
                            for s in range(2):
                                act.wait_ge(k_in[s], (b * NPAIR + a) * 64)
                        last = nc.scalar.copy(kn_hi[:, cols], j_ps[:])
                    if kind == "q":
                        for s in range(2):
                            rows = slice(s * HD_B, (s + 1) * HD_B)
                            last = nc.scalar.copy(q2[rows, a % 2, s, cols], j_ps[rows, :])
                    if kind == "v":
                        last = nc.scalar.copy(v2[:, 2 * i:2 * i + 2, :, 0:HD_B], j_ps[:].rearrange("p (t h e) -> p t h e", t=2, h=4))
                    last.then_inc(job_hi, 1)

                def exps(b, k, t, fresh):
                    keys = (2 * unit(k)[1] + t + 1) * P
                    act.wait_ge(nmx_done, (b * UNITS + k) * 2 + (t + 1))
                    if not fresh:
                        act.wait_ge(pt_ready, banks_before(*before(b, k)))
                    nc.scalar.activation(prob[:, k % 2, t, 0:keys], s_ps[t][:, 0:keys], ACT.Exp, bias=nmx[:, k % 2, t:t + 1],
                                         scale=SCALE_B, accum_out=psum_of[:, k % 2, t:t + 1]).then_inc(exp_done, 1)

                def split_pt(b, k, i):
                    act.wait_ge(pt_ready, banks_before(b, k) + (i + 1))
                    nc.scalar.copy(pt_hi[:, 2 * i:2 * i + 2, :], bank_of(k, i)[:]).then_inc(pt_hi_done, 1)

                def out(b, k, fresh):
                    K = b * UNITS + k
                    u = unit(k)[1]
                    s = unit(k)[0] % 2
                    rows = slice(s * HD_B, (s + 1) * HD_B)
                    act.wait_ge(pv_done, K + 1)
                    if s == 0 and not fresh:
                        act.wait_ge(o_done, b * (NPAIR * NU) + (unit(k)[0] // 2 - 1) * NU + (u + 1))
                    nc.scalar.copy(oa[rows, u, :], o_ps[0:HD_B, 0:2 * P]).then_inc(o_out, 1)
                    nc.scalar.copy(ob[rows, u, :], o_ps[HD_B:P, 0:2 * P]).then_inc(o_out, 1)

                act.wait_ge(w_in, 32)
                nc.scalar.copy(w_hi[:].rearrange("p d n -> p (d n)"), w_raw[:, :WQKV]).then_inc(w_hi_done, 1)
                nc.scalar.copy(wo_hi[:].rearrange("p g n -> p (g n)"), w_raw[:, WQKV:]).then_inc(w_hi_done, 1)
                act.wait_ge(zeroed, 2)
                act.wait_ge(small_in, 48)
                nc.scalar.copy(bo[0:1, :], bo_raw[:]).then_inc(w_hi_done, 1)
                norm(0)
                for i, j in enumerate(PRO):
                    job(-1, j, i, True)
                    if i == DB - 1:
                        norm(1)
                act.wait_ge(w_lo_done, 3)
                for t in range(2):
                    exps(0, 0, t, True)

                def body(b, first, last):
                    steps, _ = plan(b, first, last)
                    for k in range(UNITS):
                        jobs = list(steps[k])
                        if jobs:
                            job(b, *jobs.pop(0)[:2])
                        split_pt(b, k, 0)
                        more = not (last and k == UNITS - 1)
                        if more:
                            exps(*after(b, k), 0, first and k == 0)
                        for j in jobs:
                            job(b, *j[:2])
                        if more:
                            exps(*after(b, k), 1, first and k == 0)
                        for i in range(1, unit(k)[1] + 1):
                            split_pt(b, k, i)
                        if not (first and k == 0):
                            out(*before(b, k), first and k <= 2 * NU)
                        if not last and k in (22, 24):
                            norm((b + 1) * BC + (k - 22) // 2)

                sequences(act, body)
                out(B - 1, UNITS - 1, False)

            @block.vector
            def _(dve):
                def ln_stats(n, fresh):
                    if not fresh:
                        dve.wait_ge(rstd_done, n)
                    for j in range(CT):
                        nc.vector.bn_stats(stats[:, j, :], x_sb[:, dyn(n * CT + j), :]).then_inc(stats_done, 1)
                    wait_apart(nc, dve, c, stats_done, n * CT + CT)
                    for j in range(CT):
                        nc.vector.bn_aggr(mv[:, j, :], stats[:, j, :]).then_inc(mv_done, 1)

                def job(b, j, number, split_number):
                    kind, a, i = j
                    if kind == "y":
                        dve.wait_ge(j_ready, number + 1)
                    else:
                        dve.wait_ge(job_hi, split_number + 1)
                    cols = slice(i * CW, (i + 1) * CW)
                    if kind == "x":
                        last = nc.vector.tensor_tensor(xt_lo[:, a, i, :], j_ps[:], xt_hi[:, a, i, :].bitcast(F32), ALU.subtract)
                    if kind == "k":
                        last = nc.vector.tensor_tensor(kn_lo[:, cols], j_ps[:], kn_hi[:, cols].bitcast(F32), ALU.subtract)
                    if kind == "q":
                        for s in range(2):
                            rows, other = slice(s * HD_B, (s + 1) * HD_B), slice((1 - s) * HD_B, (2 - s) * HD_B)
                            last = nc.vector.tensor_tensor(q2[other, a % 2, s, cols], j_ps[rows, :], q2[rows, a % 2, s, cols].bitcast(F32), ALU.subtract)
                    if kind == "v":
                        last = nc.vector.tensor_tensor(v2[:, 2 * i:2 * i + 2, :, HD_B:], j_ps[:].rearrange("p (t h e) -> p t h e", t=2, h=4),
                                                       v2[:, 2 * i:2 * i + 2, :, 0:HD_B].bitcast(F32), ALU.subtract)
                    if kind == "y":
                        xs = x_sb[:, dyn((b if a >= 0 else b - 1) * BT + 2 * i, 2), :]
                        last = nc.vector.tensor_tensor(xs, j_ps[:].rearrange("p (t d) -> p t d", t=2), xs, ALU.add)
                    last.then_inc(j_done, 1)

                def maxima(b, k, t):
                    K = b * UNITS + k
                    h, u = unit(k)
                    tile = 2 * u + t
                    done = (K * 2 + t) * 2
                    far = max(tile - 1, 0) * P
                    near = slice(far, (tile + 1) * P)
                    dve.wait_ge(s_ready, K * 2 + (t + 1))
                    if far:
                        nc.vector.tensor_reduce(mx[:, t, 1:2], s_ps[t][:, 0:far], AX.X, ALU.max).then_inc(mx_step, 1)
                    else:
                        nc.vector.memset(mx[:, t, 1:2], LOWEST).then_inc(mx_step, 1)
                    nc.vector.tensor_tensor_reduce(out=s_ps[t][:, near], in0=s_ps[t][:, near], in1=bias[:, h, NEAR - (tile + 1) * P + far:], op0=ALU.add,
                                                   op1=ALU.max, scale=1.0, scalar=LOWEST, accum_out=mx[:, t, 0:1]).then_inc(mx_step, 1)
                    dve.wait_ge(mx_step, done + 2)
                    nc.vector.tensor_scalar(nmx[:, k % 2, t:t + 1], mx[:, t, 0:1], mx[:, t, 1:2], -SCALE_B, ALU.max, ALU.mult).then_inc(nmx_done, 1)

                def reciprocals(b, k):
                    dve.wait_ge(exp_done, (b * UNITS + k) * 2 + 2)
                    nc.vector.reciprocal(rsum[:, k % 2, :], psum_of[:, k % 2, :]).then_inc(rsum_done, 1)

                def split_pt(b, k, i):
                    dve.wait_ge(pt_hi_done, banks_before(b, k) + (i + 1))
                    nc.vector.tensor_tensor(pt_lo[:, 2 * i:2 * i + 2, :], bank_of(k, i)[:], pt_hi[:, 2 * i:2 * i + 2, :].bitcast(F32),
                                            ALU.subtract).then_inc(pt_lo_done, 1)

                nc.vector.memset(bo[:].bitcast(F32), 0.0).then_inc(zeroed, 1)
                nc.vector.memset(pick[:].bitcast(F32), 0.0).then_inc(zeroed, 1)
                nc.vector.memset(zeros[:], 0.0).then_inc(set_up, 1)
                ln_stats(0, True)
                dve.wait_ge(zeroed, 2)
                for r in (0, 32):
                    last = nc.vector.memset(pick[r:r + 1, :].bitcast(F32), 1.0)
                last.then_inc(set_up, 1)
                dve.wait_ge(small_in, 48)
                nc.vector.tensor_copy(rel_wide, rel[:].unsqueeze(2).to_broadcast([BUCKETS + 1, H_B, P])).then_inc(rel_done, 1)
                for h in range(H_B):
                    lo = (h // 2 % 2) * CW
                    dve.wait_ge(band_ready, h + 1)
                    nc.vector.tensor_copy(band[h], s_ps[h % 2][:, lo:lo + SPAN]).then_inc(band_done, 1)
                for i, (hi, lo, raw) in enumerate(((w_hi, w_lo, w_raw[:, :WQKV]), (wo_hi, wo_lo, w_raw[:, WQKV:]))):
                    flat = lambda x: x[:].rearrange("p d n -> p (d n)")
                    dve.wait_ge(w_hi_done, i + 1)
                    nc.vector.tensor_tensor(flat(lo), raw, flat(hi).bitcast(F32), ALU.subtract).then_inc(w_lo_done, 1)
                dve.wait_ge(w_hi_done, 3)
                nc.vector.tensor_tensor(bo[32:33, :], bo_raw[:], bo[0:1, :].bitcast(F32), ALU.subtract).then_inc(w_lo_done, 1)
                ln_stats(1, False)
                for i, j in enumerate(PRO):
                    job(-1, j, i, i)
                dve.wait_ge(bias_in, 16 * H_B)
                for t in range(2):
                    maxima(0, 0, t)

                def body(b, first, last):
                    steps, _ = plan(b, first, last)
                    for k in range(UNITS):
                        jobs = list(steps[k])
                        more = not (last and k == UNITS - 1)
                        reciprocals(b, k)
                        if more:
                            maxima(*after(b, k), 0)
                        if jobs:
                            job(b, *jobs.pop(0))
                        split_pt(b, k, 0)
                        if more:
                            maxima(*after(b, k), 1)
                        for j in jobs:
                            job(b, *j)
                        for i in range(1, unit(k)[1] + 1):
                            split_pt(b, k, i)
                        if not last and k in (20, 22):
                            ln_stats((b + 1) * BC + (k - 20) // 2, False)

                sequences(dve, body)
                for j, number in TAIL:
                    job(B - 1, j, number, None)

            @block.gpsimd
            def _(pool):
                def carry(tile):
                    nc.gpsimd.tensor_tensor(tile[:], c.eps[:, 0:1], c.eps[:, 0:1], ALU.add)

                def ln_rstd(n, fresh):
                    if not fresh:
                        pool.wait_ge(xn_done, n * CT)
                    pool.wait_ge(mv_done, n * CT + CT)
                    nc.gpsimd.tensor_tensor(veps[:], mv[:, :, 1], c.eps[:], ALU.add).then_inc(pool_step, 1)
                    pool.wait_ge(pool_step, n * 3 + 1)
                    nc.gpsimd.tensor_tensor(rstd[:], veps[:], c.minus_half[:], ALU.pow).then_inc(pool_step, 1)
                    pool.wait_ge(pool_step, n * 3 + 2)
                    nc.gpsimd.tensor_tensor(mr[:], mv[:, :, 0], rstd[:], ALU.mult).then_inc(pool_step, 1)
                    pool.wait_ge(pool_step, n * 3 + 3)
                    nc.gpsimd.tensor_tensor(nmr[:], mr[:], c.minus_one[:], ALU.mult).then_inc(rstd_done, 1)

                def normalise(b, k):
                    K = b * UNITS + k
                    pool.wait_ge(rsum_done, K + 1)
                    if not (isinstance(K, int) and K == 0):
                        pool.wait_ge(norm_done, K * 2)
                    carry(norm_carrier)
                    for t in range(2):
                        pr = prob[:, k % 2, t, 0:(2 * unit(k)[1] + t + 1) * P]
                        nc.gpsimd.tensor_scalar(pr, pr, rsum[:, k % 2, t:t + 1], 1.0, ALU.mult, ALU.mult).then_inc(norm_done, 1)

                def combine(b, k, y_number):
                    u = unit(k)[1]
                    G = b * (NPAIR * NU) + (k // (2 * NU) * NU + u)
                    cols = slice(u * 2 * P, (u + 1) * 2 * P)
                    pool.wait_ge(o_out, (b * UNITS + k) * 2 + 2)
                    if not (isinstance(G, int) and G == 0):
                        pool.wait_ge(o_done, G)
                    nc.gpsimd.tensor_tensor(osum[:], oa[:, u, :], ob[:, u, :], ALU.add).then_inc(o_step, 1)
                    pool.wait_ge(o_step, G * 2 + 1)
                    if y_number is not None:
                        pool.wait_ge(j_ready, y_number + 1)
                    carry(sum_carrier)
                    nc.gpsimd.tensor_scalar(o_hi[:, cols], osum[:], 1.0, 1.0, ALU.mult, ALU.mult).then_inc(o_step, 1)
                    pool.wait_ge(o_step, G * 2 + 2)
                    nc.gpsimd.tensor_tensor(o_lo[:, cols], osum[:], o_hi[:, cols].bitcast(F32), ALU.subtract).then_inc(o_done, 1)

                ln_rstd(0, True)
                ln_rstd(1, False)

                def body(b, first, last):
                    _, number = plan(b, first, last)

                    for k in range(UNITS):
                        normalise(b, k)
                        pb, pk = before(*before(b, k))
                        if unit(pk)[0] % 2 and not (first and k < 2):
                            p, u = pk // (2 * NU) if k >= 2 else -1, unit(pk)[1]
                            combine(pb, pk, None if first and p == 0 else number["y", p - 1, max(u, 1) if p == 0 else u])
                        if not last and k in (21, 23):
                            ln_rstd((b + 1) * BC + (k - 21) // 2, False)

                sequences(pool, body)
                for k in (UNITS - 2, UNITS - 1):
                    combine(B - 1, k, LAST_NUMBER["y", NPAIR - 2, unit(k)[1]])

        m.clear_sems()


class Consts:
    pass


def build(nc, dram):
    x_view = dram["x"].rearrange("(t p) d -> p t d", p=P)
    out_view = dram["out"].rearrange("(t p) d -> p t d", p=P)
    with ExitStack() as ctx:
        m = Mem(nc, ctx, "all")
        x_sb = m.sb("x", [P, T, D])
        c = Consts()
        c.ident = m.sb("ident", [P, P])
        c.iota8 = m.sb("iota8", [P, E])
        c.minus_half = m.sb("minus_half", [P, CT])
        c.minus_one = m.sb("minus_one", [P, CT])
        c.eps = m.sb("eps", [P, CT])
        c.carrier = m.sb("carrier", [P, 1])
        loaded = m.sem("loaded")
        made = m.sem("made")
        with nc.Block() as block:

            @block.sync
            def _(sp):
                sp.dma_start(c.ident[:], dram["ident"]).then_inc(loaded, 16)
                sp.dma_start(c.iota8[:], dram["iota8"]).then_inc(loaded, 16)
                for b in range(B):
                    t = b * N // P
                    sp.dma_start(x_sb[:, t:t + N // P, :], x_view[:, t:t + N // P, :]).then_inc(loaded, 16)
                sp.wait_ge(loaded, 16 * (2 + B))

            @block.vector
            def _(dve):
                for tile, value in ((c.minus_half, -0.5), (c.minus_one, -1.0), (c.eps, EPS_LN)):
                    nc.vector.memset(tile[:], value).then_inc(made, 1)
                dve.wait_ge(made, 3)

        linear_attention_stage(nc, x_sb, c, dram)
        ffn_stage(nc, "f1", x_sb, c, dram)
        softmax_attention_stage(nc, x_sb, c, dram)
        ffn_stage(nc, "f2", x_sb, c, dram, out_view)


def by_dist():
    n = NEAR - 1 - np.arange(SPAN)
    exact = BUCKETS // 2
    large = exact + (np.log(np.maximum(n, 1).astype(np.float32) / np.float32(exact)) / np.float32(math.log(MAX_DIST / exact))
                     * np.float32(BUCKETS - exact)).astype(np.int32)
    bucket = np.where(n < exact, np.maximum(n, 0), np.minimum(large, BUCKETS - 1))
    table = np.zeros((BUCKETS + 1, SPAN), np.float32)
    for col in range(SPAN):
        if n[col] >= 0:
            table[bucket[col], col] += 1 / SCALE_B ** 2
            table[BUCKETS - 1, col] -= 1 / SCALE_B ** 2
        else:
            table[BUCKETS, col] = MASKED
    return table


def layouts(v):
    a = {k: np.asarray(x) for k, x in v.items()}
    gate, up, downw = a["L0_ffn_Wg"], a["L0_ffn_Wu"], a["L0_ffn_Wd"]
    w_ffn = np.empty((NFB, P, FBW), np.float32)
    for fb in range(NFB):
        if fb < NSH:
            cols = slice(fb * F, (fb + 1) * F)
            g, u, d = a["L0_ffn_Sg"][:, cols], a["L0_ffn_Su"][:, cols], a["L0_ffn_Sd"][cols]
        else:
            g, u, d = gate[fb - NSH], up[fb - NSH], downw[fb - NSH]
        for k in range(DB):
            w_ffn[fb, :, k * 2 * F:k * 2 * F + F] = g[k * P:(k + 1) * P]
            w_ffn[fb, :, k * 2 * F + F:(k + 1) * 2 * F] = u[k * P:(k + 1) * P]
        w_ffn[fb, :, 2 * D:] = d
    out = {
        "x": a["L0_attn_a_x"].reshape(B * N, D),
        "w_qkv_a": np.concatenate([a[f"L0_attn_a_W{k}"].T.reshape(DB, P, D).transpose(1, 0, 2) for k in "qkv"], axis=2),
        "b_q_a": a["L0_attn_a_bq"].reshape(DB, P).T,
        "b_kv_a": np.concatenate([a["L0_attn_a_bk"], a["L0_attn_a_bv"]]).reshape(1, 2 * D),
        "gamma": a["L0_attn_a_gamma"].reshape(1, D),
        "beta": a["L0_attn_a_beta"].reshape(1, D),
        "head_mask": np.kron(np.eye(HB_A, dtype=np.float32), np.ones((HD_A, HD_A), np.float32)),
        "head_of": np.kron(np.eye(HB_A, dtype=np.float32), np.ones((HD_A, 1), np.float32)),
        "w_qkv_b": np.concatenate([a["L0_attn_b_Wq"], a["L0_attn_b_Wkv"]], axis=1).reshape(DB, P, 3 * INNER).transpose(1, 0, 2).reshape(P, -1),
        "w_o_b": a["L0_attn_b_Wo"].reshape(NPAIR, P, D).transpose(1, 0, 2).reshape(P, -1),
        "b_o_b": np.tile(a["L0_attn_b_bo"].reshape(1, D), (1, 2)),
        "rel_emb": np.concatenate([a["L0_attn_b_rel_emb"], np.ones((1, H_B), np.float32)]),
        "by_dist": by_dist(),
        "w_ffn": w_ffn,
        "w_router": a["L0_ffn_Wr"].reshape(DB, P, E).transpose(1, 0, 2),
        "expert_bias": a["L0_ffn_expert_bias"].reshape(E, 1),
        "ident": np.eye(P, dtype=np.float32),
        "iota8": np.tile(np.arange(E, dtype=np.float32), (P, 1)),
    }
    return {k: np.ascontiguousarray(x) for k, x in out.items()}


def kernel(**inputs):
    import concourse.bacc as bacc
    from concourse.bass_utils import run_bass_kernel_spmd

    nc = bacc.Bacc("TRN2", target_bir_lowering=False, num_devices=1)
    arrays = {f"in_{k}": x for k, x in layouts(inputs).items()}
    dram = {k[3:]: nc.dram_tensor(k, x.shape, mybir.dt.from_np(x.dtype), kind="ExternalInput").ap() for k, x in arrays.items()}
    dram["out"] = nc.dram_tensor("out", (B * N, D), F32, kind="ExternalOutput").ap()
    build(nc, dram)
    r = run_bass_kernel_spmd(nc, [arrays], core_ids=[0])
    return r.results[0]["out"].reshape(B, N, D)
```

```python
import math
from contextlib import ExitStack

import numpy as np

import concourse.bass as bass
from concourse import mybir

F32 = mybir.dt.float32
F32R = mybir.dt.float32r
U32 = mybir.dt.uint32
ALU = mybir.AluOpType
ACT = mybir.ActivationFunctionType
AX = mybir.AxisListType

P = 128
D = 256
DB = D // P
B, N = 4, 1024
T = B * N // P
CT = 4
CW = CT * P
NCH = T // CT
EPS_LN = 1e-5

E, F, FS = 8, 128, 256
NSH = FS // F
NFB = NSH + E
FBW = 2 * D + D


def dyn(i, size=1):
    return slice(i, i + size) if isinstance(i, int) else bass.ds(i, size)


def loop(nc, eng, start, end):
    return nc.Fori(start, end, engines=[eng.engine], hint_back_edge=True)


def wait_apart(nc, eng, c, sem, value):
    eng.wait_ge(sem, value)
    nc.vector.memset(c.carrier[:], 0.0)


class Mem:

    def __init__(self, nc, ctx, tag):
        self.nc, self.ctx, self.tag, self.sems = nc, ctx, tag, []

    def sb(self, name, shape, dt=F32):
        return self.ctx.enter_context(self.nc.sbuf_tensor(f"{self.tag}_{name}", shape, dt))

    def ps(self, name, shape, dt=F32):
        return self.ctx.enter_context(self.nc.psum_tensor(f"{self.tag}_{name}", shape, dt))

    def sem(self, name):
        self.sems.append(self.nc.alloc_semaphore(name=f"{self.tag}_{name}"))
        return self.sems[-1]

    def clear_sems(self):
        self.nc.clear_and_free_semaphores(self.sems)
        self.nc.all_engine_barrier()


def ffn_stage(nc, tag, x_sb, c, dram, out_view=None):
    with ExitStack() as ctx:
        m = Mem(nc, ctx, tag)
        RAW = 4
        w_raw = m.sb("w_raw", [P, RAW, FBW])
        w_hi = m.sb("w_hi", [P, NFB, FBW], F32R)
        w_lo = m.sb("w_lo", [P, NFB, FBW], F32R)
        wr_raw = m.sb("wr_raw", [P, DB, E])
        wr_hi = m.sb("wr_hi", [P, DB, E], F32R)
        wr_lo = m.sb("wr_lo", [P, DB, E], F32R)
        ebias = m.sb("ebias", [E, 1])
        stats = m.sb("stats", [P, CT, 6])
        mv = m.sb("mv", [P, CT, 2])
        veps = m.sb("veps", [P, CT])
        rstd = m.sb("rstd", [P, CT])
        mr = m.sb("mr", [P, CT])
        nmr = m.sb("nmr", [P, CT])
        carrier = m.sb("carrier", [P, 1])
        xn = m.sb("xn", [P, CT, D])
        xt_hi = m.sb("xt_hi", [P, 2, DB, CW], F32R)
        xt_lo = m.sb("xt_lo", [P, 2, DB, CW], F32R)
        lg = m.sb("lg", [E, CW])
        top = m.sb("top", [P, CT, 8])
        topi = m.sb("topi", [P, CT, 8], U32)
        topf = m.sb("topf", [P, CT, 2])
        gap = m.sb("gap", [P, CT])
        th = m.sb("th", [P, CT])
        prob = m.sb("prob", [P, CT, 2])
        hot1 = m.sb("hot1", [P, CT, E])
        hot2 = m.sb("hot2", [P, CT, E])
        pr1 = m.sb("pr1", [P, CT, E])
        pr2 = m.sb("pr2", [P, CT, E])
        rw = m.sb("rw", [P, CT, E])
        rwt = m.sb("rwt", [E, CW])
        rw_row = m.sb("rw_row", [1, E, CW])
        rw_bc = m.sb("rw_bc", [P, E, CW])
        sil = m.sb("sil", [P, 2, CW])
        su = m.sb("su", [P, 2, CW])
        hid = m.sb("hid", [P, 2, CW])
        h_hi = m.sb("h_hi", [P, 5, CW], F32R)
        h_lo = m.sb("h_lo", [P, 5, CW], F32R)
        ot = m.sb("ot", [P, DB, CW])
        g_ps = [m.ps(f"g{i}", [P, CW]) for i in range(2)]
        u_ps = [m.ps(f"u{i}", [P, CW]) for i in range(2)]
        o_ps = [m.ps(f"o{i}", [P, CW]) for i in range(DB)]
        t_ps = [m.ps(f"t{i}", [P, CW]) for i in range(2)]

        w_in = [m.sem(f"w_in{i}") for i in range(NFB)]
        wr_in, wr_hi_done, wr_lo_done = m.sem("wr_in"), m.sem("wr_hi_done"), m.sem("wr_lo_done")
        w_hi_done, w_lo_done = m.sem("w_hi_done"), m.sem("w_lo_done")
        stats_done, mv_done = m.sem("stats_done"), m.sem("mv_done")
        pool_step, rstd_done, xn_done = m.sem("pool_step"), m.sem("rstd_done"), m.sem("xn_done")
        xt_ready, xt_hi_done, xt_lo_done = m.sem("xt_ready"), m.sem("xt_hi_done"), m.sem("xt_lo_done")
        lg_ready, lg_done, lgt_ready = m.sem("lg_ready"), m.sem("lg_done"), m.sem("lgt_ready")
        top_done, dve_step, gap_done, th_done = m.sem("top_done"), m.sem("dve_step"), m.sem("gap_done"), m.sem("th_done")
        rw_done, rwt_ready, rwt_done = m.sem("rw_done"), m.sem("rwt_ready"), m.sem("rwt_done")
        row_done, bc_done = m.sem("row_done"), m.sem("bc_done")
        g_ready, u_ready, sil_done, mul_done = m.sem("g_ready"), m.sem("u_ready"), m.sem("sil_done"), m.sem("mul_done")
        rwmul_done, hi_done, lo_done, down_done = m.sem("rwmul_done"), m.sem("hi_done"), m.sem("lo_done"), m.sem("down_done")
        ot0_done, ot1_done, back_ready, y_added = m.sem("ot0_done"), m.sem("ot1_done"), m.sem("back_ready"), m.sem("y_added")
        stored = m.sem("stored")

        EARLY = 6

        def chunks(eng, body, tail):
            body(0, 0, True, False)
            with loop(nc, eng, 0, (NCH - 2) // 2) as i:
                body(i * 2 + 1, 1, False, False)
                body(i * 2 + 2, 0, False, False)
            body(NCH - 1, 1, False, True)
            tail()

        with nc.Block() as block:

            @block.sync
            def _(sp):
                for fb in range(NFB):
                    if fb >= RAW:
                        sp.wait_ge(w_lo_done, fb - RAW + 1)
                    sp.dma_start(w_raw[:, fb % RAW, :], dram["w_ffn"][fb]).then_inc(w_in[fb], 16)
                    if fb == 0:
                        sp.dma_start(wr_raw[:], dram["w_router"]).then_inc(wr_in, 16)
                        sp.dma_start(ebias[:], dram["expert_bias"]).then_inc(wr_in, 16)

                def row(n):
                    sp.wait_ge(rwt_done, n + 1)
                    if not isinstance(n, int) or n > 0:
                        sp.wait_ge(bc_done, n * E)
                    sp.dma_start(rw_row[0:1, :, :], rwt[:, :]).then_inc(row_done, 16)

                def store(n):
                    sp.wait_ge(y_added, n * 2 + 2)
                    sp.dma_start(out_view[:, dyn(n * CT, CT), :], x_sb[:, dyn(n * CT, CT), :]).then_inc(stored, 16)

                row(0)
                with loop(nc, sp, 0, NCH - 1) as i:
                    row(i + 1)
                    if out_view is not None:
                        store(i)
                if out_view is not None:
                    store(NCH - 1)
                    sp.wait_ge(stored, 16 * NCH)

            @block.tensor
            def _(pe):
                def transposes(n, par):
                    pe.wait_ge(xn_done, n * CT + CT)
                    for d in range(DB):
                        for j in range(CT):
                            last = nc.tensor.transpose(t_ps[d][:, j * P:(j + 1) * P], xn[:, j, d * P:(d + 1) * P], c.ident[:])
                        last.then_inc(xt_ready, 1)

                def router(n, par):
                    pe.wait_ge(xt_hi_done, n * DB + DB)
                    pe.wait_ge(xt_lo_done, n * DB + DB)
                    k = 0
                    for d in range(DB):
                        for w, xt in ((wr_hi, xt_hi), (wr_hi, xt_lo), (wr_lo, xt_hi)):
                            last = nc.tensor.matmul(t_ps[0][0:E, :], w[:, d, :], xt[:, par, d, :], start=(k == 0), stop=(k == 5))
                            k += 1
                    last.then_inc(lg_ready, 1)

                def logits_back(n):
                    for j in range(CT):
                        last = nc.tensor.transpose(t_ps[1][:, j * E:(j + 1) * E], lg[:, j * P:(j + 1) * P], c.ident[0:E, 0:E])
                    last.then_inc(lgt_ready, 1)

                def weights_over(n):
                    pe.wait_ge(rw_done, n + 1)
                    for j in range(CT):
                        last = nc.tensor.transpose(t_ps[0][0:E, j * P:(j + 1) * P], rw[:, j, :], c.ident[:])
                    last.then_inc(rwt_ready, 1)

                def gate_up(n, par, fb, first):
                    if first:
                        pe.wait_ge(w_hi_done, fb + 1)
                        pe.wait_ge(w_lo_done, fb + 1)
                    fresh = first and fb < 2
                    for ps, off, free, ready in ((g_ps, 0, sil_done, g_ready), (u_ps, F, mul_done, u_ready)):
                        if not fresh:
                            pe.wait_ge(free, n * NFB + (fb - 1))
                        k = 0
                        for d in range(DB):
                            lo = d * 2 * F + off
                            for w, xt in ((w_hi, xt_hi), (w_hi, xt_lo), (w_lo, xt_hi)):
                                last = nc.tensor.matmul(ps[fb % 2][:], w[:, fb, lo:lo + F], xt[:, par, d, :], start=(k == 0), stop=(k == 5))
                                k += 1
                        last.then_inc(ready, 1)

                def down(n, fb):
                    pe.wait_ge(hi_done, n * NFB + (fb + 1))
                    pe.wait_ge(lo_done, n * NFB + (fb + 1))
                    if fb == 0 and (not isinstance(n, int) or n > 0):
                        pe.wait_ge(ot0_done, n)
                        pe.wait_ge(ot1_done, n)
                    for d in range(DB):
                        lo = 2 * D + d * P
                        for k, (w, h) in enumerate(((w_hi, h_hi), (w_hi, h_lo), (w_lo, h_hi))):
                            last = nc.tensor.matmul(o_ps[d][:], w[:, fb, lo:lo + P], h[:, fb % 5, :],
                                                    start=(fb == 0 and k == 0), stop=(fb == NFB - 1 and k == 2))
                    last.then_inc(down_done, 1)

                def back(n):
                    pe.wait_ge(ot0_done, n + 1)
                    pe.wait_ge(ot1_done, n + 1)
                    for h in range(2):
                        for jj in range(2):
                            j = 2 * h + jj
                            for d in range(DB):
                                last = nc.tensor.transpose(t_ps[h][:, jj * D + d * P:jj * D + (d + 1) * P], ot[:, d, j * P:(j + 1) * P], c.ident[:])
                        last.then_inc(back_ready, 1)

                transposes(0, 0)
                pe.wait_ge(wr_hi_done, 1)
                pe.wait_ge(wr_lo_done, 1)
                router(0, 0)
                pe.wait_ge(lg_done, 1)
                logits_back(0)

                def body(n, par, first, last):
                    for fb in range(NFB):
                        gate_up(n, par, fb, first)
                        if fb == 0 and first:
                            weights_over(0)
                        if fb == 2 and not first:
                            pe.wait_ge(rwt_done, n + 1)
                            pe.wait_ge(top_done, n + 1)
                            back(n - 1)
                        if fb == 4 and not last:
                            if first:
                                pe.wait_ge(rwt_done, 1)
                                pe.wait_ge(top_done, 1)
                            else:
                                pe.wait_ge(y_added, n * 2)
                            transposes(n + 1, 1 - par)
                        if fb == 5 and not last:
                            router(n + 1, 1 - par)
                        if fb == 6 and not last:
                            pe.wait_ge(lg_done, n + 2)
                        if fb == 9 and not last:
                            weights_over(n + 1)
                        if fb >= 2:
                            down(n, fb - 2)
                        elif not first:
                            down(n - 1, NFB - 2 + fb)
                        if fb == 6 and not last:
                            logits_back(n + 1)

                def tail():
                    down(NCH - 1, NFB - 2)
                    down(NCH - 1, NFB - 1)
                    back(NCH - 1)

                chunks(pe, body, tail)

            @block.scalar
            def _(act):
                def split_w(fb):
                    act.wait_ge(w_in[fb], 16)
                    nc.scalar.copy(w_hi[:, fb, :], w_raw[:, fb % RAW, :]).then_inc(w_hi_done, 1)

                def norm(n):
                    act.wait_ge(rstd_done, n + 1)
                    if not isinstance(n, int) or n > 0:
                        act.wait_ge(xt_ready, n * DB)
                    for j in range(CT):
                        nc.scalar.activation(xn[:, j:j + 1, :], x_sb[:, dyn(n * CT + j), :], ACT.Identity,
                                             bias=nmr[:, j:j + 1], scale=rstd[:, j:j + 1]).then_inc(xn_done, 1)

                def split_xt(n, par):
                    for d in range(DB):
                        act.wait_ge(xt_ready, n * DB + (d + 1))
                        nc.scalar.copy(xt_hi[:, par, d, :], t_ps[d][:]).then_inc(xt_hi_done, 1)

                def logits(n):
                    act.wait_ge(lg_ready, n + 1)
                    if not isinstance(n, int) or n > 0:
                        act.wait_ge(lgt_ready, n)
                    nc.scalar.activation(lg[:], t_ps[0][0:E, :], ACT.Identity, bias=ebias[:, 0:1]).then_inc(lg_done, 1)

                def half_tanh(n):
                    act.wait_ge(gap_done, n + 1)
                    nc.scalar.activation(th[:], gap[:], ACT.Tanh, scale=0.5).then_inc(th_done, 1)

                def weights_out(n):
                    act.wait_ge(rwt_ready, n + 1)
                    if not isinstance(n, int) or n > 0:
                        act.wait_ge(row_done, n * 16)
                    nc.scalar.copy(rwt[:], t_ps[0][0:E, :]).then_inc(rwt_done, 1)

                def silu(n, fb, first):
                    act.wait_ge(g_ready, n * NFB + (fb + 1))
                    if not (first and fb < 2):
                        act.wait_ge(mul_done, n * NFB + (fb - 1))
                    nc.scalar.activation(sil[:, fb % 2, :], g_ps[fb % 2][:], ACT.Silu).then_inc(sil_done, 1)

                def hi(n, fb, first):
                    if fb < NSH:
                        act.wait_ge(mul_done, n * NFB + (fb + 1))
                    else:
                        act.wait_ge(rwmul_done, n * E + (fb - NSH + 1))
                    if not (first and fb < 5):
                        act.wait_ge(down_done, n * NFB + (fb - 4))
                    nc.scalar.copy(h_hi[:, fb % 5, :], hid[:, fb % 2, :]).then_inc(hi_done, 1)

                def out_evac(n):
                    act.wait_ge(down_done, n * NFB + NFB)
                    if not isinstance(n, int) or n > 0:
                        act.wait_ge(back_ready, n * 2)
                    nc.scalar.copy(ot[:, 0, :], o_ps[0][:]).then_inc(ot0_done, 1)

                act.wait_ge(wr_in, 32)
                nc.scalar.copy(wr_hi[:], wr_raw[:]).then_inc(wr_hi_done, 1)
                split_w(0)
                norm(0)
                split_w(1)
                split_xt(0, 0)
                logits(0)
                for fb in range(2, 4):
                    split_w(fb)
                half_tanh(0)
                for fb in range(4, EARLY):
                    split_w(fb)
                weights_out(0)

                def body(n, par, first, last):
                    for fb in range(NFB):
                        silu(n, fb, first)
                        if fb >= 1:
                            hi(n, fb - 1, first)
                        if first and fb + EARLY < NFB:
                            split_w(fb + EARLY)
                        if fb == 1 and not first:
                            out_evac(n - 1)
                        if not last:
                            if fb == 2:
                                norm(n + 1)
                            if fb == 4:
                                split_xt(n + 1, 1 - par)
                            if fb == 6:
                                logits(n + 1)
                            if fb == 7:
                                half_tanh(n + 1)
                    hi(n, NFB - 1, first)
                    if not last:
                        weights_out(n + 1)

                def tail():
                    out_evac(NCH - 1)

                chunks(act, body, tail)

            @block.vector
            def _(dve):
                def split_w(fb):
                    dve.wait_ge(w_hi_done, fb + 1)
                    nc.vector.tensor_tensor(w_lo[:, fb, :], w_raw[:, fb % RAW, :], w_hi[:, fb, :].bitcast(F32), ALU.subtract).then_inc(w_lo_done, 1)

                def ln_stats(n):
                    if not isinstance(n, int) or n > 0:
                        dve.wait_ge(rstd_done, n)
                    for j in range(CT):
                        ins = nc.vector.bn_stats(stats[:, j, :], x_sb[:, dyn(n * CT + j), :])
                        ins.then_inc(stats_done, 1)
                    wait_apart(nc, dve, c, stats_done, n * CT + CT)
                    for j in range(CT):
                        nc.vector.bn_aggr(mv[:, j, :], stats[:, j, :]).then_inc(mv_done, 1)

                def split_xt(n, par):
                    for d in range(DB):
                        dve.wait_ge(xt_hi_done, n * DB + (d + 1))
                        nc.vector.tensor_tensor(xt_lo[:, par, d, :], t_ps[d][:], xt_hi[:, par, d, :].bitcast(F32), ALU.subtract).then_inc(xt_lo_done, 1)

                STEPS = 14

                def route_top(n):
                    s = n * STEPS
                    wait_apart(nc, dve, c, lgt_ready, n + 1)
                    for j in range(CT):
                        nc.vector.max(top[:, j, :], t_ps[1][:, j * E:(j + 1) * E]).then_inc(dve_step, 1)
                    wait_apart(nc, dve, c, dve_step, s + 4)
                    for j in range(CT):
                        ins = nc.vector.max_index(topi[:, j, :], top[:, j, :], t_ps[1][:, j * E:(j + 1) * E])
                        ins.then_inc(dve_step, 1)
                    nc.vector.tensor_tensor(gap[:], top[:, :, 0], top[:, :, 1], ALU.subtract).then_inc(gap_done, 1)
                    dve.wait_ge(dve_step, s + 8)
                    nc.vector.tensor_copy(topf[:], topi[:, :, 0:2]).then_inc(top_done, 1)
                    dve.wait_ge(top_done, n + 1)
                    for k, hot in ((0, hot1), (1, hot2)):
                        nc.vector.tensor_tensor(hot[:], c.iota8[:].unsqueeze(1).to_broadcast([P, CT, E]),
                                                topf[:, :, k:k + 1].to_broadcast([P, CT, E]), ALU.is_equal).then_inc(dve_step, 1)

                def route_weights(n):
                    s = n * STEPS
                    dve.wait_ge(th_done, n + 1)
                    nc.vector.tensor_scalar(prob[:, :, 0], th[:], 0.5, 0.5, ALU.mult, ALU.add).then_inc(dve_step, 1)
                    nc.vector.tensor_scalar(prob[:, :, 1], th[:], -0.5, 0.5, ALU.mult, ALU.add).then_inc(dve_step, 1)
                    dve.wait_ge(dve_step, s + 12)
                    for k, hot, pr in ((0, hot1, pr1), (1, hot2, pr2)):
                        nc.vector.tensor_tensor(pr[:], hot[:], prob[:, :, k:k + 1].to_broadcast([P, CT, E]), ALU.mult).then_inc(dve_step, 1)
                    dve.wait_ge(dve_step, s + 14)
                    if not isinstance(n, int) or n > 0:
                        dve.wait_ge(rwt_ready, n)
                    nc.vector.tensor_tensor(rw[:], pr1[:], pr2[:], ALU.add).then_inc(rw_done, 1)

                def mul(n, fb, first):
                    k = n * NFB
                    dve.wait_ge(sil_done, k + (fb + 1))
                    dve.wait_ge(u_ready, k + (fb + 1))
                    if fb < NSH:
                        if not first:
                            dve.wait_ge(lo_done, k + (fb - 1))
                        out = hid[:, fb % 2, :]
                    else:
                        if fb >= NSH + 2:
                            dve.wait_ge(rwmul_done, n * E + (fb - NSH - 1))
                        elif not first:
                            dve.wait_ge(rwmul_done, n * E)
                        out = su[:, fb % 2, :]
                    nc.vector.tensor_tensor(out, u_ps[fb % 2][:], sil[:, fb % 2, :], ALU.mult).then_inc(mul_done, 1)

                def lo(n, fb, first):
                    dve.wait_ge(hi_done, n * NFB + (fb + 1))
                    if not (first and fb < 5):
                        dve.wait_ge(down_done, n * NFB + (fb - 4))
                    nc.vector.tensor_tensor(h_lo[:, fb % 5, :], hid[:, fb % 2, :], h_hi[:, fb % 5, :].bitcast(F32), ALU.subtract).then_inc(lo_done, 1)

                def out_evac(n):
                    dve.wait_ge(down_done, n * NFB + NFB)
                    if not isinstance(n, int) or n > 0:
                        dve.wait_ge(back_ready, n * 2)
                    nc.vector.tensor_copy(ot[:, 1, :], o_ps[1][:]).then_inc(ot1_done, 1)

                def add(n):
                    for h in range(2):
                        dve.wait_ge(back_ready, n * 2 + (h + 1))
                        xs = x_sb[:, dyn(n * CT + 2 * h, 2), :]
                        nc.vector.tensor_tensor(xs, t_ps[h][:].rearrange("p (j d) -> p j d", j=2), xs, ALU.add).then_inc(y_added, 1)

                ln_stats(0)
                dve.wait_ge(wr_hi_done, 1)
                nc.vector.tensor_tensor(wr_lo[:], wr_raw[:], wr_hi[:].bitcast(F32), ALU.subtract).then_inc(wr_lo_done, 1)
                split_w(0)
                split_w(1)
                split_xt(0, 0)
                route_top(0)
                for fb in range(2, 4):
                    split_w(fb)
                route_weights(0)
                for fb in range(4, EARLY):
                    split_w(fb)

                def body(n, par, first, last):
                    for fb in range(NFB):
                        mul(n, fb, first)
                        if fb >= 1:
                            lo(n, fb - 1, first)
                        if first and fb + EARLY < NFB:
                            split_w(fb + EARLY)
                        if fb == 1 and not first:
                            out_evac(n - 1)
                        if fb == 0 and not last:
                            ln_stats(n + 1)
                        if fb == 3 and not first:
                            add(n - 1)
                        if not last:
                            if fb == 4:
                                split_xt(n + 1, 1 - par)
                            if fb == 7:
                                route_top(n + 1)
                            if fb == 8:
                                route_weights(n + 1)
                    lo(n, NFB - 1, first)

                def tail():
                    out_evac(NCH - 1)
                    add(NCH - 1)

                chunks(dve, body, tail)

            @block.gpsimd
            def _(pool):
                def ln_rstd(n):
                    s = n * 3
                    if not isinstance(n, int) or n > 0:
                        pool.wait_ge(xn_done, n * CT)
                    pool.wait_ge(mv_done, n * CT + CT)
                    nc.gpsimd.tensor_tensor(veps[:], mv[:, :, 1], c.eps[:], ALU.add).then_inc(pool_step, 1)
                    pool.wait_ge(pool_step, s + 1)
                    nc.gpsimd.tensor_tensor(rstd[:], veps[:], c.minus_half[:], ALU.pow).then_inc(pool_step, 1)
                    pool.wait_ge(pool_step, s + 2)
                    nc.gpsimd.tensor_tensor(mr[:], mv[:, :, 0], rstd[:], ALU.mult).then_inc(pool_step, 1)
                    pool.wait_ge(pool_step, s + 3)
                    nc.gpsimd.tensor_tensor(nmr[:], mr[:], c.minus_one[:], ALU.mult).then_inc(rstd_done, 1)

                def broadcast(n):
                    if not isinstance(n, int) or n > 0:
                        pool.wait_ge(rwmul_done, n * E)
                    pool.wait_ge(row_done, n * 16 + 16)
                    nc.gpsimd.tensor_tensor(carrier[:], c.eps[:, 0:1], c.eps[:, 0:1], ALU.add)
                    for e in range(E):
                        nc.gpsimd.partition_broadcast(rw_bc[:, e, :], rw_row[0:1, e, :], P).then_inc(bc_done, 1)

                def weigh(n, fb, first):
                    pool.wait_ge(mul_done, n * NFB + (fb + 1))
                    pool.wait_ge(bc_done, n * E + (fb - NSH + 1))
                    pool.wait_ge(lo_done, n * NFB + (fb - 1))
                    nc.gpsimd.tensor_tensor(hid[:, fb % 2, :], su[:, fb % 2, :], rw_bc[:, fb - NSH, :], ALU.mult).then_inc(rwmul_done, 1)

                ln_rstd(0)
                broadcast(0)

                def body(n, par, first, last):
                    if not last:
                        ln_rstd(n + 1)
                    for fb in range(NSH, NFB):
                        weigh(n, fb, first)
                    if not last:
                        broadcast(n + 1)

                chunks(pool, body, lambda: None)

        m.clear_sems()


H_A = 16
HD_A = D // H_A
HB_A = P // HD_A
BC = N // CW
BT = N // P
KVW = P + 2 + P
EPS_DEN = 1e-6


def linear_attention_stage(nc, x_sb, c, dram):
    with ExitStack() as ctx:
        m = Mem(nc, ctx, "a")
        w_raw = m.sb("w_raw", [P, DB, 3 * D])
        w_hi = m.sb("w_hi", [P, DB, 3 * D], F32R)
        w_lo = m.sb("w_lo", [P, DB, 3 * D], F32R)
        bq = m.sb("bq", [P, DB])
        bkv_raw = m.sb("bkv_raw", [1, 2 * D])
        bkv = m.sb("bkv", [P, 2 * D], F32R)
        pick = m.sb("pick", [P, P], F32R)
        gamma = m.sb("gamma", [P, D])
        beta = m.sb("beta", [P, D])
        head_mask = m.sb("head_mask", [P, P])
        head_of = m.sb("head_of", [P, HB_A])
        stats = m.sb("stats", [P, CT, 6])
        mv = m.sb("mv", [P, CT, 2])
        veps, rstd, mr, nmr = (m.sb(s, [P, CT]) for s in ("veps", "rstd", "mr", "nmr"))
        xn = m.sb("xn", [P, BT, D])
        xt_hi = m.sb("xt_hi", [P, 2, DB, CW], F32R)
        xt_lo = m.sb("xt_lo", [P, 2, DB, CW], F32R)
        qf = m.sb("qf", [P, 2, CW])
        q_hi = m.sb("q_hi", [P, BC, DB, CW], F32R)
        q_lo = m.sb("q_lo", [P, BC, DB, CW], F32R)
        k_hi = m.sb("k_hi", [P, 2, D], F32R)
        k_lo = m.sb("k_lo", [P, 2, D], F32R)
        v2 = m.sb("v2", [P, 2, DB, KVW], F32R)
        kv_part = m.sb("kv_part", [P, DB, P])
        kv_sum = m.sb("kv_sum", [P, DB, P])
        mix = m.sb("mix", [P, DB, D])
        mix_hi = m.sb("mix_hi", [P, DB, D], F32R)
        mix_lo = m.sb("mix_lo", [P, DB, D], F32R)
        den = m.sb("den", [P, 2, DB, HB_A])
        rden = m.sb("rden", [P, 2, DB, HB_A])
        att = m.sb("att", [P, 2, 2, D])
        y = m.sb("y", [P, BT, D])
        ystats = m.sb("ystats", [P, CT, 6])
        ymv = m.sb("ymv", [P, CT, 2])
        yveps, yrstd, ymr, ynmr = (m.sb(s, [P, CT]) for s in ("yveps", "yrstd", "ymr", "ynmr"))
        yn = m.sb("yn", [P, CT, D])
        yg = m.sb("yg", [P, CT, D])
        yb = m.sb("yb", [P, CT, D])
        t_ps = [m.ps(f"t{i}", [P, CW]) for i in range(2)]
        p_ps = [m.ps(f"p{i}", [P, 2 * D]) for i in range(2)]
        kv_ps = [m.ps(f"kv{i}", [P, 2 * D]) for i in range(DB)]
        cx_ps = [m.ps(f"cx{i}", [P, DB, D])[:] for i in range(2)] + [ps[:].rearrange("p (j d) -> p j d", j=DB) for ps in p_ps]

        w_in, small_in, x_in = m.sem("w_in"), m.sem("small_in"), m.sem("x_in")
        w_hi_done, w_lo_done, zeroed, set_up = m.sem("w_hi_done"), m.sem("w_lo_done"), m.sem("zeroed"), m.sem("set_up")
        stats_done, mv_done, pool_step = m.sem("stats_done"), m.sem("mv_done"), m.sem("pool_step")
        rstd_done, xn_done = m.sem("rstd_done"), m.sem("xn_done")
        xt_ready, xt_hi_done, xt_lo_done = m.sem("xt_ready"), m.sem("xt_hi_done"), m.sem("xt_lo_done")
        q_ready, qf_done, q_hi_done, q_lo_done = m.sem("q_ready"), m.sem("qf_done"), m.sem("q_hi_done"), m.sem("q_lo_done")
        p_ready, kv_hi_done, kv_lo_done, kvacc_done = m.sem("p_ready"), m.sem("kv_hi_done"), m.sem("kv_lo_done"), m.sem("kvacc_done")
        part_done, mix_step, mix_hi_done, mix_lo_done = m.sem("part_done"), m.sem("mix_step"), m.sem("mix_hi_done"), m.sem("mix_lo_done")
        cx_ready, out_step, att_done, y_done = m.sem("cx_ready"), m.sem("out_step"), m.sem("att_done"), m.sem("y_done")
        ystats_done, ymv_done, ypool_step, yrstd_done = m.sem("ystats_done"), m.sem("ymv_done"), m.sem("ypool_step"), m.sem("yrstd_done")
        yn_done, yg_done, yb_done, x_added = m.sem("yn_done"), m.sem("yg_done"), m.sem("yb_done"), m.sem("x_added")

        def sequences(eng, body):
            body(0, True, False)
            with loop(nc, eng, 1, B - 1) as b:
                body(b, False, False)
            body(B - 1, False, True)

        CHUNK_AT = 1

        with nc.Block() as block:

            @block.sync
            def _(sp):
                sp.dma_start(w_raw[:], dram["w_qkv_a"]).then_inc(w_in, 16)
                sp.dma_start(bkv_raw[:], dram["b_kv_a"]).then_inc(w_in, 16)
                for tile, name in ((bq, "b_q_a"), (head_mask, "head_mask"), (head_of, "head_of")):
                    sp.dma_start(tile[:], dram[name]).then_inc(small_in, 16)
                for tile, name in ((gamma, "gamma"), (beta, "beta")):
                    sp.dma_start(tile[:], dram[name].to_broadcast([P, D])).then_inc(small_in, 16)
                x_view = dram["x"].rearrange("(t p) d -> p t d", p=P)
                sp.dma_start(x_sb[:, BT:, :], x_view[:, BT:, :]).then_inc(x_in, 16)

            @block.tensor
            def _(pe):
                def transposes(n, c_, fresh):
                    pe.wait_ge(xn_done, n * CT + CT)
                    if not fresh:
                        pe.wait_ge(qf_done, n * DB)
                    for d in range(DB):
                        for j in range(CT):
                            last = nc.tensor.transpose(t_ps[d][:, j * P:(j + 1) * P], xn[:, c_ * CT + j, d * P:(d + 1) * P], c.ident[:])
                        last.then_inc(xt_ready, 1)

                def queries(n, c_):
                    pe.wait_ge(xt_hi_done, n * DB + DB)
                    pe.wait_ge(xt_lo_done, n * DB + DB)
                    for o in range(DB):
                        k = 0
                        for d in range(DB):
                            for w, xt in ((w_hi, xt_hi), (w_hi, xt_lo), (w_lo, xt_hi)):
                                last = nc.tensor.matmul(t_ps[o][:], w[:, d, o * P:(o + 1) * P], xt[:, c_, d, :], start=(k == 0), stop=(k == 5))
                                k += 1
                        last.then_inc(q_ready, 1)

                def keys_values(t, i, fresh):
                    if not fresh:
                        pe.wait_ge(kv_lo_done, (t - 1) * 2)
                        if i < 2:
                            pe.wait_ge(att_done, t - i)
                    ps = p_ps[i % 2]
                    nc.tensor.matmul(ps[:], pick[:], bkv[:], start=True, stop=False)
                    cols = slice((i % CT) * P, (i % CT + 1) * P)
                    for d in range(DB):
                        for xt, w in ((xt_hi, w_hi), (xt_hi, w_lo), (xt_lo, w_hi)):
                            last = nc.tensor.matmul(ps[:], xt[:, i // CT, d, cols], w[:, d, D:], start=False, stop=(d == 1 and xt is xt_lo))
                    last.then_inc(p_ready, 1)

                def accumulate(t, i):
                    pe.wait_ge(kv_lo_done, t * 2 + 2)
                    for j in range(DB):
                        for k in (k_hi, k_lo):
                            last = nc.tensor.matmul(kv_ps[j][:, 0:KVW], k[:, i % 2, j * P:(j + 1) * P], v2[:, i % 2, j, :],
                                                    start=(i == 0 and k is k_hi), stop=(i == BT - 1 and k is k_lo))
                    last.then_inc(kvacc_done, 1)

                def context(t, i, fresh):
                    if not fresh:
                        pe.wait_ge(att_done, t - 3)
                    cols = slice((i % CT) * P, (i % CT + 1) * P)
                    for j in range(DB):
                        for k, (q, w) in enumerate(((q_hi, mix_hi), (q_hi, mix_lo), (q_lo, mix_hi))):
                            last = nc.tensor.matmul(cx_ps[i % 4][:, j, :], q[:, i // CT, j, cols], w[:, j, :], start=(k == 0), stop=(k == 2))
                    last.then_inc(cx_ready, 1)

                pe.wait_ge(set_up, 2)
                pe.wait_ge(w_lo_done, 2)

                def body(b, first, last):
                    n, t = b * BC, b * BT
                    transposes(n, 0, first)
                    queries(n, 0)
                    for i in range(BT):
                        if i == CT:
                            pe.wait_ge(xt_lo_done, n * DB + 2 * DB)
                        keys_values(t + i, i, first and i < 2)
                        if i >= 1:
                            accumulate(t + (i - 1), i - 1)
                        if i == CHUNK_AT:
                            transposes(n + 1, 1, False)
                    accumulate(t + (BT - 1), BT - 1)
                    queries(n + 1, 1)
                    pe.wait_ge(mix_hi_done, b + 1)
                    pe.wait_ge(mix_lo_done, b + 1)
                    for i in range(BT):
                        if i % CT == 0:
                            pe.wait_ge(q_hi_done, n * DB + (i // CT + 1) * DB)
                            pe.wait_ge(q_lo_done, n * DB + (i // CT + 1) * DB)
                        context(t + i, i, first and i < 4)

                sequences(pe, body)

            @block.scalar
            def _(act):
                def norm(n, c_, fresh):
                    act.wait_ge(rstd_done, n + 1)
                    if not fresh:
                        act.wait_ge(y_done, (n - 1) * CT)
                    for j in range(CT):
                        nc.scalar.activation(xn[:, c_ * CT + j:c_ * CT + j + 1, :], x_sb[:, dyn(n * CT + j), :], ACT.Identity,
                                             bias=nmr[:, j:j + 1], scale=rstd[:, j:j + 1]).then_inc(xn_done, 1)

                def split_xt(n, c_):
                    for d in range(DB):
                        act.wait_ge(xt_ready, n * DB + (d + 1))
                        nc.scalar.copy(xt_hi[:, c_, d, :], t_ps[d][:]).then_inc(xt_hi_done, 1)

                def split_q(n, c_):
                    for o in range(DB):
                        act.wait_ge(qf_done, n * DB + (o + 1))
                        nc.scalar.copy(q_hi[:, c_, o, :], qf[:, o, :]).then_inc(q_hi_done, 1)

                def split_kv(t, i, fresh):
                    act.wait_ge(p_ready, t + 1)
                    if not fresh:
                        act.wait_ge(kvacc_done, t - 1)
                    ps = p_ps[i % 2]
                    nc.scalar.activation(k_hi[:, i % 2, :], ps[:, 0:D], ACT.Relu).then_inc(kv_hi_done, 1)
                    nc.scalar.copy(v2[:, i % 2, :, 0:P], ps[:, D:].rearrange("p (j v) -> p j v", j=DB)).then_inc(kv_hi_done, 1)

                def normalise_y(n, c_):
                    act.wait_ge(yrstd_done, n + 1)
                    if c_ == 1:
                        act.wait_ge(yg_done, n)
                    for j in range(CT):
                        nc.scalar.activation(yn[:, j, :], y[:, c_ * CT + j, :], ACT.Identity, bias=ynmr[:, j:j + 1],
                                             scale=yrstd[:, j:j + 1]).then_inc(yn_done, 1)

                act.wait_ge(w_in, 32)
                nc.scalar.copy(w_hi[:], w_raw[:]).then_inc(w_hi_done, 1)
                act.wait_ge(zeroed, 3)
                nc.scalar.copy(bkv[0:1, :], bkv_raw[:]).then_inc(w_hi_done, 1)
                norm(0, 0, True)

                def body(b, first, last):
                    n, t = b * BC, b * BT
                    split_xt(n, 0)
                    if not first:
                        normalise_y(n - BC, 0)
                    split_q(n, 0)
                    for i in range(BT):
                        split_kv(t + i, i, first and i < 2)
                        if i == 0:
                            norm(n + 1, 1, first)
                        if i == CHUNK_AT:
                            split_xt(n + 1, 1)
                        if i == 2 and not first:
                            normalise_y(n - 1, 1)
                    act.wait_ge(kvacc_done, t + BT)
                    for j in range(DB):
                        nc.scalar.copy(kv_part[:, j, :], kv_ps[j][:, P + 2:KVW]).then_inc(part_done, 1)
                    act.wait_ge(mix_step, b * 6 + 6)
                    nc.scalar.copy(mix_hi[:], mix[:]).then_inc(mix_hi_done, 1)
                    split_q(n + 1, 1)
                    if not last:
                        norm(n + BC, 0, False)
                    if last:
                        normalise_y(n, 0)

                sequences(act, body)
                normalise_y(NCH - 1, 1)

            @block.vector
            def _(dve):
                def ln_stats(n, fresh):
                    if not fresh:
                        dve.wait_ge(rstd_done, n)
                    for j in range(CT):
                        nc.vector.bn_stats(stats[:, j, :], x_sb[:, dyn(n * CT + j), :]).then_inc(stats_done, 1)
                    wait_apart(nc, dve, c, stats_done, n * CT + CT)
                    for j in range(CT):
                        nc.vector.bn_aggr(mv[:, j, :], stats[:, j, :]).then_inc(mv_done, 1)

                def split_xt(n, c_):
                    for d in range(DB):
                        dve.wait_ge(xt_hi_done, n * DB + (d + 1))
                        nc.vector.tensor_tensor(xt_lo[:, c_, d, :], t_ps[d][:], xt_hi[:, c_, d, :].bitcast(F32), ALU.subtract).then_inc(xt_lo_done, 1)

                def relu_q(n, fresh):
                    for o in range(DB):
                        dve.wait_ge(q_ready, n * DB + (o + 1))
                        if not fresh:
                            dve.wait_ge(q_hi_done, (n - 1) * DB + (o + 1))
                            dve.wait_ge(q_lo_done, (n - 1) * DB + (o + 1))
                        nc.vector.tensor_scalar(qf[:, o, :], t_ps[o][:], bq[:, o:o + 1], 0.0, ALU.add, ALU.max).then_inc(qf_done, 1)

                def split_kv(t, i):
                    ps = p_ps[i % 2]
                    dve.wait_ge(kv_hi_done, t * 2 + 2)
                    nc.vector.scalar_tensor_tensor(out=k_lo[:, i % 2, :], in0=ps[:, 0:D], scalar=0.0, in1=k_hi[:, i % 2, :].bitcast(F32),
                                                   op0=ALU.max, op1=ALU.subtract).then_inc(kv_lo_done, 1)
                    nc.vector.tensor_tensor(v2[:, i % 2, :, P + 2:], ps[:, D:].rearrange("p (j v) -> p j v", j=DB),
                                            v2[:, i % 2, :, 0:P].bitcast(F32), ALU.subtract).then_inc(kv_lo_done, 1)

                nc.vector.memset(bkv[:].bitcast(F32), 0.0).then_inc(zeroed, 1)
                nc.vector.memset(pick[:].bitcast(F32), 0.0).then_inc(zeroed, 1)
                nc.vector.memset(mix[:], 0.0).then_inc(zeroed, 1)
                nc.vector.memset(v2[:, :, :, P:P + 2].bitcast(F32), 1.0).then_inc(set_up, 1)
                ln_stats(0, True)
                dve.wait_ge(zeroed, 3)
                for r in (0, 32):
                    last = nc.vector.memset(pick[r:r + 1, :].bitcast(F32), 1.0)
                last.then_inc(set_up, 1)
                dve.wait_ge(w_hi_done, 1)
                nc.vector.tensor_tensor(w_lo[:], w_raw[:], w_hi[:].bitcast(F32), ALU.subtract).then_inc(w_lo_done, 1)
                dve.wait_ge(w_hi_done, 2)
                nc.vector.tensor_tensor(bkv[32:33, :], bkv_raw[:], bkv[0:1, :].bitcast(F32), ALU.subtract).then_inc(w_lo_done, 1)
                dve.wait_ge(small_in, 16 * 5)

                def attend(b, t, g, first):
                    i, s = 2 * g, b * (BT // 2) + g
                    for k in range(2):
                        dve.wait_ge(cx_ready, t + (i + k + 1))
                        nc.vector.tensor_scalar(den[:, k], cx_ps[(i + k) % 4][:, :, P:P + HB_A], EPS_DEN, None, ALU.max).then_inc(out_step, 1)
                    dve.wait_ge(out_step, s * 3 + 2)
                    nc.vector.reciprocal(rden[:], den[:]).then_inc(out_step, 1)
                    dve.wait_ge(out_step, s * 3 + 3)
                    if not (first and g < 2):
                        dve.wait_ge(y_done, t + (i - 2))
                    for k in range(2):
                        nc.vector.tensor_tensor(att[:, g % 2, k, :].rearrange("p (j h e) -> p j h e", j=DB, h=HB_A),
                                                cx_ps[(i + k) % 4][:, :, 0:P].rearrange("p j (h e) -> p j h e", h=HB_A),
                                                rden[:, k].unsqueeze(3).to_broadcast([P, DB, HB_A, HD_A]), ALU.mult).then_inc(att_done, 1)

                def y_stats(n, t, g, first):
                    h = 2 * g // CT
                    dve.wait_ge(y_done, t + (2 * g + 2))
                    for k in range(2):
                        nc.vector.bn_stats(ystats[:, (2 * g + k) % CT, :], y[:, 2 * g + k, :]).then_inc(ystats_done, 1)
                    if (2 * g + 2) % CT == 0:
                        if not (first and h == 0):
                            dve.wait_ge(yrstd_done, n + h)
                        wait_apart(nc, dve, c, ystats_done, t + (h * CT + CT))
                        for j in range(CT):
                            nc.vector.bn_aggr(ymv[:, j, :], ystats[:, j, :]).then_inc(ymv_done, 1)

                def add(n):
                    xs = x_sb[:, dyn(n * CT, CT), :]
                    dve.wait_ge(yg_done, n + 1)
                    if not (isinstance(n, int) and n == 0):
                        dve.wait_ge(x_added, n)
                    nc.vector.tensor_tensor(yb[:], yg[:], beta[:].unsqueeze(1).to_broadcast([P, CT, D]), ALU.add).then_inc(yb_done, 1)
                    dve.wait_ge(yb_done, n + 1)
                    nc.vector.tensor_tensor(xs, xs, yb[:], ALU.add).then_inc(x_added, 1)

                ADD_AT = (2, 4)

                def body(b, first, last):
                    n, t = b * BC, b * BT
                    split_xt(n, 0)
                    ln_stats(n + 1, False)
                    if not first:
                        y_stats(n - BC, t - BT, BT // 2 - 1, False)
                    relu_q(n, first)
                    for i in range(BT):
                        split_kv(t + i, i)
                        if i == CHUNK_AT:
                            split_xt(n + 1, 1)
                        if i in ADD_AT and not first:
                            add(n - BC + ADD_AT.index(i))
                        if i == 5 and not last:
                            if first:
                                dve.wait_ge(x_in, 16)
                            ln_stats(n + BC, False)
                    dve.wait_ge(kvacc_done, t + BT)
                    if not first:
                        dve.wait_ge(mix_lo_done, b)
                    for j in range(DB):
                        dve.wait_ge(part_done, b * DB + (j + 1))
                        nc.vector.tensor_tensor(kv_sum[:, j, :], kv_ps[j][:, 0:P], kv_part[:, j, :], ALU.add).then_inc(mix_step, 1)
                        nc.vector.tensor_scalar(mix[:, j, P:P + HB_A], head_of[:], kv_ps[j][:, P:P + 1], None, ALU.mult).then_inc(mix_step, 1)
                    dve.wait_ge(mix_step, b * 6 + 4)
                    for j in range(DB):
                        nc.vector.tensor_tensor(mix[:, j, 0:P], kv_sum[:, j, :], head_mask[:], ALU.mult).then_inc(mix_step, 1)
                    dve.wait_ge(mix_hi_done, b + 1)
                    nc.vector.tensor_tensor(mix_lo[:], mix[:], mix_hi[:].bitcast(F32), ALU.subtract).then_inc(mix_lo_done, 1)
                    relu_q(n + 1, False)
                    for g in range(BT // 2):
                        attend(b, t, g, first)
                        if g >= 1:
                            y_stats(n, t, g - 1, first)
                    if last:
                        y_stats(n, t, BT // 2 - 1, first)

                sequences(dve, body)
                for n in range(NCH - BC, NCH):
                    dve.wait_ge(yn_done, n * CT + CT)
                    dve.wait_ge(yb_done, n)
                    nc.vector.tensor_tensor(yg[:], yn[:], gamma[:].unsqueeze(1).to_broadcast([P, CT, D]), ALU.mult).then_inc(yg_done, 1)
                    add(n)

            @block.gpsimd
            def _(pool):
                def rstd_of(n, mv, veps, rstd, mr, nmr, ready, step, done, read, fresh):
                    if not fresh:
                        pool.wait_ge(read, n * CT)
                    pool.wait_ge(ready, n * CT + CT)
                    nc.gpsimd.tensor_tensor(veps[:], mv[:, :, 1], c.eps[:], ALU.add).then_inc(step, 1)
                    pool.wait_ge(step, n * 3 + 1)
                    nc.gpsimd.tensor_tensor(rstd[:], veps[:], c.minus_half[:], ALU.pow).then_inc(step, 1)
                    pool.wait_ge(step, n * 3 + 2)
                    nc.gpsimd.tensor_tensor(mr[:], mv[:, :, 0], rstd[:], ALU.mult).then_inc(step, 1)
                    pool.wait_ge(step, n * 3 + 3)
                    nc.gpsimd.tensor_tensor(nmr[:], mr[:], c.minus_one[:], ALU.mult).then_inc(done, 1)

                def ln_rstd(n, fresh):
                    rstd_of(n, mv, veps, rstd, mr, nmr, mv_done, pool_step, rstd_done, xn_done, fresh)

                def split_q(n, c_):
                    for o in range(DB):
                        pool.wait_ge(q_hi_done, n * DB + (o + 1))
                        nc.gpsimd.tensor_tensor(q_lo[:, c_, o, :], qf[:, o, :], q_hi[:, c_, o, :].bitcast(F32), ALU.subtract).then_inc(q_lo_done, 1)

                ln_rstd(0, True)
                pool.wait_ge(small_in, 16 * 5)

                def y_rstd(n, fresh):
                    rstd_of(n, ymv, yveps, yrstd, ymr, ynmr, ymv_done, ypool_step, yrstd_done, yn_done, fresh)

                def scale_y(n, fresh):
                    pool.wait_ge(yn_done, n * CT + CT)
                    if not fresh:
                        pool.wait_ge(yb_done, n)
                    nc.gpsimd.tensor_tensor(yg[:], yn[:], gamma[:].unsqueeze(1).to_broadcast([P, CT, D]), ALU.mult).then_inc(yg_done, 1)

                def residual(t, g, first):
                    i = 2 * g
                    pool.wait_ge(att_done, t + (i + 2))
                    if not first:
                        pool.wait_ge(yn_done, t - BT + (i // CT + 1) * CT)
                    nc.gpsimd.tensor_tensor(y[:, i:i + 2, :], att[:, g % 2], xn[:, i:i + 2, :], ALU.add).then_inc(y_done, 2)

                def body(b, first, last):
                    n, t = b * BC, b * BT
                    ln_rstd(n + 1, False)
                    if not first:
                        y_rstd(n - 1, False)
                    if not first:
                        scale_y(n - 1, False)
                    split_q(n, 0)
                    if not last:
                        ln_rstd(n + BC, False)
                    split_q(n + 1, 1)
                    for g in range(BT // 2):
                        if g == BT // 2 - 1:
                            y_rstd(n, first)
                        residual(t, g, first)
                    if not last:
                        scale_y(n, first)

                sequences(pool, body)
                y_rstd(NCH - 1, False)

        m.clear_sems()


H_B, HD_B = 8, 64
INNER = H_B * HD_B
NPAIR = H_B // 2
NU = BT // 2
UNITS = H_B * NU
BUCKETS, MAX_DIST = 32, 128
NEAR = 2 * P
SPAN = 3 * P
MASKED = -1e30
SCALE_B = HD_B ** -0.5
LOWEST = -3e38


def softmax_attention_stage(nc, x_sb, c, dram):
    with ExitStack() as ctx:
        m = Mem(nc, ctx, "b")
        prob = m.sb("prob", [P, 2, 2, N])
        w_raw = prob[:].rearrange("p a t k -> p (a t k)")
        WQKV = DB * 3 * INNER
        w_hi = m.sb("w_hi", [P, DB, 3 * INNER], F32R)
        w_lo = m.sb("w_lo", [P, DB, 3 * INNER], F32R)
        wo_hi = m.sb("wo_hi", [P, NPAIR, D], F32R)
        wo_lo = m.sb("wo_lo", [P, NPAIR, D], F32R)
        bo = m.sb("bo", [P, 2 * D], F32R)
        pick = m.sb("pick", [P, P], F32R)
        rel = m.sb("rel", [BUCKETS + 1, H_B])
        by_dist = m.sb("by_dist", [BUCKETS + 1, SPAN])
        bias = m.sb("bias", [P, H_B, NEAR])
        zeros = m.sb("zeros", [P, P])
        stats = m.sb("stats", [P, CT, 6])
        mv = m.sb("mv", [P, CT, 2])
        veps, rstd, mr, nmr = (m.sb(s, [P, CT]) for s in ("veps", "rstd", "mr", "nmr"))
        xn = m.sb("xn", [P, CT, D])
        xt_hi = m.sb("xt_hi", [P, BC, DB, CW], F32R)
        xt_lo = m.sb("xt_lo", [P, BC, DB, CW], F32R)
        q2 = m.sb("q2", [P, 2, 2, N], F32R)
        kn_hi = m.sb("kn_hi", [P, N], F32R)
        kn_lo = m.sb("kn_lo", [P, N], F32R)
        k_hi2 = m.sb("k_hi2", [P, 2, N], F32R)
        k_lo2 = m.sb("k_lo2", [P, 2, N], F32R)
        v2 = m.sb("v2", [P, BT, 4, 2 * HD_B], F32R)
        mx = m.sb("mx", [P, 2, 2])
        nmx = m.sb("nmx", [P, 2, 2])
        psum_of = m.sb("psum_of", [P, 2, 2])
        rsum = m.sb("rsum", [P, 2, 2])
        pt_hi = m.sb("pt_hi", [P, BT, 2 * P], F32R)
        pt_lo = m.sb("pt_lo", [P, BT, 2 * P], F32R)
        oa = m.sb("oa", [P, NU, 2 * P])
        ob = m.sb("ob", [P, NU, 2 * P])
        rb = m.sb("rb", [P, NU, 2 * P])
        osum = m.sb("osum", [P, 2 * P])
        bo_raw = rb[0:1, 0:2, :].rearrange("p a b -> p (a b)")
        band = [part[:].rearrange("p a b -> p (a b)")[:, i * SPAN:(i + 1) * SPAN] for part, n in ((bias, 5), (ob, 2)) for i in range(n)] + [rb[:, 2:4, :].rearrange("p a b -> p (a b)")[:, 0:SPAN]]
        rel_wide = oa[0:BUCKETS + 1].rearrange("p u q -> p (u q)").rearrange("p (h q) -> p h q", h=H_B)
        o_hi = m.sb("o_hi", [P, N], F32R)
        o_lo = m.sb("o_lo", [P, N], F32R)
        carrier = m.sb("carrier", [P, 1])
        band_dram = nc.dram_tensor("band_scratch", (H_B, P, SPAN), F32, kind="Internal").ap()
        s_ps = [m.ps(f"s{i}", [P, N]) for i in range(2)]
        pt_ps = [m.ps(f"pt{i}", [P, 2, 2 * P]) for i in range(2)]
        o_ps = m.ps("o", [P, 2 * P * 2])
        j_ps = m.ps("j", [P, CW])

        w_in, small_in, zeroed, set_up = m.sem("w_in"), m.sem("small_in"), m.sem("zeroed"), m.sem("set_up")
        w_hi_done, w_lo_done = m.sem("w_hi_done"), m.sem("w_lo_done")
        rel_done, band_ready, band_done, band_out, bias_in = (m.sem(s) for s in ("rel_done", "band_ready", "band_done", "band_out", "bias_in"))
        stats_done, mv_done, pool_step, rstd_done, xn_done = (m.sem(s) for s in ("stats_done", "mv_done", "pool_step", "rstd_done", "xn_done"))
        j_ready, job_hi, j_done = m.sem("j_ready"), m.sem("job_hi"), m.sem("j_done")
        k_in = [m.sem(f"k_in{s}") for s in range(2)]
        s_ready, mx_step, nmx_done, exp_done, rsum_done = (m.sem(s) for s in ("s_ready", "mx_step", "nmx_done", "exp_done", "rsum_done"))
        pt_ready, pt_hi_done, pt_lo_done, pv_done = (m.sem(s) for s in ("pt_ready", "pt_hi_done", "pt_lo_done", "pv_done"))
        o_out, o_step, o_done = m.sem("o_out"), m.sem("o_step"), m.sem("o_done")

        TRI = [u * (u + 1) // 2 for u in range(NU + 1)]
        BANKS = H_B * TRI[NU]

        STATS_AT, RSTD_AT, NORM_AT = (UNITS - 11, UNITS - 9), (UNITS - 10, UNITS - 8), (UNITS - 9, UNITS - 7)

        def unit(k):
            return k // NU, k % NU

        def banks_before(b, k):
            return b * BANKS + ((k // NU) * TRI[NU] + TRI[k % NU])

        def bank_of(k, i):
            h, u = unit(k)
            return pt_ps[(h * TRI[NU] + TRI[u] + i) % 2]

        JOBS_AT = [["X0", ""], ["X1", "y1"], ["X2", "q0"], ["k0", "X3"], ["q1", ""], ["k1", ""], ["y3", ""], ["y2", "y0"]]

        def jobs_at(k, first, last):
            p, r = k // (2 * NU), k % (2 * NU)
            if p % 2 == 0:
                new = [("v", p // 2, i) for i in range(NU)]
            else:
                new = [("x", n, d) for n in range(BC) for d in range(DB)] if p == NPAIR - 1 and not last else [None] * 4
            y = [("y", p - 1, u) for u in range(NU)] if not (first and p == 0) else [None] * NU
            ahead = not (last and p == NPAIR - 1)
            kq = [(kind, p + 1, i) if ahead else None for kind in "kq" for i in range(BC)]
            named = {"": None, "y0": ("y", p, 0), "k0": kq[0], "k1": kq[1], "q0": kq[2], "q1": kq[3]}
            for i in range(NU):
                named["X" + str(i)] = new[i]
                if i:
                    named["y" + str(i)] = y[i]
            return tuple(named[name] for name in JOBS_AT[r])

        ACT_ORDER = [["h01"], ["0h", "h1"], ["h0", "h", "1h"], ["h", "0h", "1h", "h"]]
        DVE_ORDER = [["01l"], ["01l", "l"], ["0l", "1l", "l"], ["01l", "l", "l", "l"]]
        SECOND_AFTER = [0, 0, 1, 1]
        JOB_AFTER = [0, 0, 1, 1]
        OUT_LATE = [False, False, False, True]

        def jobs_of(k, first, last):
            return [j for j in jobs_at(k, first, last) if j]

        def splits(jobs):
            return sum(j[0] != "y" for j in jobs)

        PRO = [("x", n, d) for n in range(BC) for d in range(DB)] + [(kind, NPAIR, n) for kind in "kq" for n in range(BC)]
        pro_ps = [j_ps[:]] + [bank[:].rearrange("p a q -> p (a q)") for bank in pt_ps] + [o_ps[:]]
        JOBS = [sum((jobs_of(k, f, False) for k in range(UNITS)), []) for f in (True, False)]

        def plan(b, first, last):
            at = len(PRO) if first else b * len(JOBS[1]) + (len(PRO) + len(JOBS[0]) - len(JOBS[1]))
            split_at = b * splits(JOBS[1]) + len(PRO)
            steps, n, ns = [], 0, 0
            number = {("y", a - NPAIR, u): at + (JOBS[1].index(("y", a, u)) - len(JOBS[1])) for a in (NPAIR - 2, NPAIR - 1) for u in range(NU)
                      if not first and ("y", a, u) in JOBS[1]}
            for k in range(UNITS):
                steps.append([])
                for j in jobs_at(k, first, last):
                    steps[-1].append(j and (j, at + n, split_at + ns))
                    if j:
                        number[j] = at + n
                        n, ns = n + 1, ns + (j[0] != "y")
            return steps, number

        LAST, LAST_NUMBER = plan(B - 1, False, True)
        TAIL_AT = (B - 1) * len(JOBS[1]) + (len(PRO) + len(JOBS[0]) - len(JOBS[1])) + sum(len(jobs_of(k, False, True)) for k in range(UNITS))
        TAIL = [(("y", NPAIR - 1, u), TAIL_AT + u - 1) for u in range(1, NU)]

        def sequences(eng, body):
            body(0, True, False)
            with loop(nc, eng, 1, B - 1) as b:
                body(b, False, False)
            body(B - 1, False, True)

        def after(b, k):
            return (b, k + 1) if k < UNITS - 1 else (b + 1, 0)

        def before(b, k):
            return (b, k - 1) if k else (b - 1, UNITS - 1)

        with nc.Block() as block:

            @block.sync
            def _(sp):
                for tile, name in ((bo_raw, "b_o_b"), (rel[:], "rel_emb"), (by_dist[:], "by_dist")):
                    sp.dma_start(tile, dram[name]).then_inc(small_in, 16)
                sp.dma_start(w_raw[:, :WQKV], dram["w_qkv_b"]).then_inc(w_in, 16)
                sp.dma_start(w_raw[:, WQKV:], dram["w_o_b"]).then_inc(w_in, 16)
                for h in range(H_B):
                    sp.wait_ge(band_done, h + 1)
                    sp.dma_start(band_dram[h], band[h]).then_inc(band_out, 16)
                sp.wait_ge(band_out, 16 * H_B)
                for h in range(H_B):
                    skewed = bass.AP(tensor=band_dram.tensor, offset=h * P * SPAN + P - 1, ap=[[SPAN - 1, P], [1, NEAR]])
                    sp.dma_start(bias[:, h, :], skewed).then_inc(bias_in, 16)

                def spread(g, number, fresh):
                    sp.wait_ge(j_done, number + 1)
                    for s in range(2):
                        if not fresh:
                            sp.wait_ge(s_ready, g * (4 * NU) + 2 * NU * (s - 1))
                        rows = slice(s * HD_B, (s + 1) * HD_B)
                        for dst, src in ((k_hi2, kn_hi), (k_lo2, kn_lo)):
                            for half in range(2):
                                sp.dma_start(dst[half * HD_B:(half + 1) * HD_B, s, :].bitcast(F32), src[rows, :].bitcast(F32)).then_inc(k_in[s], 16)

                spread(0, PRO.index(("k", NPAIR, BC - 1)), True)

                def body(b, first, last):
                    _, number = plan(b, first, last)
                    for p in range(1, NPAIR + (not last)):
                        spread(b * NPAIR + p, number["k", p, BC - 1], False)

                sequences(sp, body)

            @block.tensor
            def _(pe):
                three = lambda x, y: ((x[0], y[0]), (x[0], y[1]), (x[1], y[0]))
                xt, w = (xt_hi, xt_lo), (w_hi, w_lo)

                def scores(b, k, t, q_number, fresh):
                    K = b * UNITS + k
                    h, u = unit(k)
                    s = h % 2
                    if u == 0 and t == 0:
                        if s == 0:
                            pe.wait_ge(j_done, q_number + 1)
                        pe.wait_ge(k_in[s], (b * NPAIR + h // 2) * 64 + 64)
                    if not fresh:
                        pe.wait_ge(exp_done, K * 2 + (t - 1))
                    cols = slice((2 * u + t) * P, (2 * u + t + 1) * P)
                    width = 2 * P * (u + 1)
                    for lo in range(0, width, CW):
                        hi = min(width, lo + CW)
                        for kk in (k_hi2, k_lo2):
                            last = nc.tensor.matmul(s_ps[t][:, lo:hi], q2[:, (h // 2) % 2, s, cols], kk[:, s, lo:hi], start=kk is k_hi2, stop=kk is k_lo2)
                    last.then_inc(s_ready, 1)

                def turn(b, k, i, fresh):
                    u = unit(k)[1]
                    nb = banks_before(b, k) + i
                    if i == 0:
                        pe.wait_ge(exp_done, (b * UNITS + k) * 2 + 2)
                    if not fresh:
                        pe.wait_ge(pt_lo_done, nb - 1)
                    bank = bank_of(k, i)
                    for a in range(2):
                        kt = 2 * i + a
                        for t in range(2):
                            src = zeros[:] if kt > 2 * u + t else prob[:, k % 2, t, kt * P:(kt + 1) * P]
                            last = nc.tensor.transpose(bank[:, a, t * P:(t + 1) * P], src, c.ident[:])
                    last.then_inc(pt_ready, 1)

                def product(b, k, i, v_number, fresh):
                    u = unit(k)[1]
                    pe.wait_ge(pt_lo_done, banks_before(b, k) + (i + 1))
                    if i == 0 and not fresh:
                        pe.wait_ge(o_out, (b * UNITS + k) * 3)
                    if v_number is not None:
                        pe.wait_ge(j_done, v_number + 1)
                    for a in range(2):
                        kt = 2 * i + a
                        for pt in (pt_hi, pt_lo):
                            last = nc.tensor.matmul(o_ps[:, 0:2 * P], v2[:, kt, unit(k)[0] % 4, :], pt[:, kt, :],
                                                    start=(kt == 0 and pt is pt_hi), stop=(kt == 2 * u + 1 and pt is pt_lo))
                    if i == u:
                        pe.wait_ge(rsum_done, b * UNITS + k + 1)
                        for t in range(2):
                            last = nc.tensor.transpose(o_ps[:, (2 + t) * P:(3 + t) * P], rsum[:, k % 2, t:t + 1].to_broadcast([P, P]), c.ident[:])
                        last.then_inc(pv_done, 1)

                def job(b, j, done, bank=j_ps):
                    kind, a, i = j
                    if done is not None:
                        pe.wait_ge(j_done, done)
                    if kind == "x":
                        pe.wait_ge(xn_done, (b + 1) * (BC * CT) + (a + 1) * CT)
                        for t in range(CT):
                            last = nc.tensor.transpose(bank[:, t * P:(t + 1) * P], xn[:, t, i * P:(i + 1) * P], c.ident[:])
                    if kind in "kq":
                        lo = (INNER if kind == "k" else 0) + (a % NPAIR) * P
                        terms = [(ww[:, d, lo:lo + P], xx[:, i, d, :]) for d in range(DB) for ww, xx in three(w, xt)]
                        for n, (ww, xx) in enumerate(terms):
                            last = nc.tensor.matmul(bank[:], ww, xx, start=(n == 0), stop=(n == len(terms) - 1))
                    if kind == "v":
                        lo = 2 * INNER + a * D
                        for t in range(2):
                            kt = 2 * i + t
                            cols = slice((kt % CT) * P, (kt % CT + 1) * P)
                            terms = [(xx[:, kt // CT, d, cols], ww[:, d, lo:lo + D]) for d in range(DB) for xx, ww in three(xt, w)]
                            for n, (xx, ww) in enumerate(terms):
                                last = nc.tensor.matmul(bank[:, t * D:(t + 1) * D], xx, ww, start=(n == 0), stop=(n == len(terms) - 1))
                    if kind == "y":
                        pe.wait_ge(o_done, (b * NPAIR + a) * NU + (i + 1))
                        pair = a % NPAIR
                        if pair == 0:
                            nc.tensor.matmul(bank[:], pick[:], bo[:], start=True, stop=False)
                        for t in range(2):
                            cols = slice((2 * i + t) * P, (2 * i + t + 1) * P)
                            for n, (oo, ww) in enumerate(three((o_hi, o_lo), (wo_hi, wo_lo))):
                                last = nc.tensor.matmul(bank[:, t * D:(t + 1) * D], oo[:, cols], ww[:, pair, :],
                                                        start=(n == 0 and pair > 0), stop=(n == 2 and (pair > 0 or t == 1)))
                    last.then_inc(j_ready, 1)

                pe.wait_ge(rel_done, 1)
                pe.wait_ge(small_in, 48)
                for h in range(H_B):
                    if h >= 4:
                        pe.wait_ge(band_done, h - 3)
                    lo = (h // 2 % 2) * CW
                    nc.tensor.matmul(s_ps[h % 2][:, lo:lo + SPAN], rel_wide[:, h, :], by_dist[:], start=True, stop=True).then_inc(band_ready, 1)
                    if h % 4 == 3:
                        for i in range(h // 4 * DB, (h // 4 + 1) * DB):
                            job(-1, PRO[i], None, pro_ps[i])
                pe.wait_ge(w_lo_done, 3)
                pe.wait_ge(set_up, 2)
                for i in range(BC * DB, len(PRO)):
                    job(-1, PRO[i], BC * DB, pro_ps[i % 4])
                pe.wait_ge(band_done, H_B)
                for t in range(2):
                    scores(0, 0, t, len(PRO) - 1, True)

                def body(b, first, last):
                    steps, number = plan(b, first, last)
                    for k in range(UNITS):
                        early, late = steps[k]
                        def ahead(t):
                            if not (last and k == UNITS - 1):
                                scores(*after(b, k), t, number.get(("q", (k + 1) // (2 * NU), BC - 1)), False)

                        u = unit(k)[1]
                        ahead(0)
                        if not SECOND_AFTER[u]:
                            ahead(1)
                        pb, pk = before(b, k)
                        ph, pu = unit(pk) if not (first and k == 0) else (0, -1)
                        for i in range(max(u, pu) + 1):
                            if i <= pu:
                                product(pb, pk, i, number["v", ph // 4, i] if ph % 4 == 0 and i == pu else None, first and k == 1)
                            if i <= u:
                                turn(b, k, i, first and banks_before(0, k) + i < 2)
                            if SECOND_AFTER[u] and i == SECOND_AFTER[u] - 1:
                                ahead(1)
                            if early and i == JOB_AFTER[unit(k)[1]]:
                                job(b, *early[:2])
                        if late:
                            job(b, *late[:2])

                sequences(pe, body)
                for i in range(unit(UNITS - 1)[1] + 1):
                    product(B - 1, UNITS - 1, i, None, False)
                for j, number in TAIL:
                    job(B - 1, j, number)

            @block.scalar
            def _(act):
                def norm(n):
                    act.wait_ge(rstd_done, n + 1)
                    for j in range(CT):
                        nc.scalar.activation(xn[:, j:j + 1, :], x_sb[:, dyn(n * CT + j), :], ACT.Identity,
                                             bias=nmr[:, j:j + 1], scale=rstd[:, j:j + 1]).then_inc(xn_done, 1)

                def job(b, j, number, fresh=False, bank=j_ps):
                    kind, a, i = j
                    if kind == "y":
                        return
                    act.wait_ge(j_ready, number + 1)
                    cols = slice(i * CW, (i + 1) * CW)
                    if kind == "x":
                        last = nc.scalar.copy(xt_hi[:, a, i, :], bank[:])
                    if kind == "k":
                        if not fresh:
                            for s in range(2):
                                act.wait_ge(k_in[s], (b * NPAIR + a) * 64)
                        last = nc.scalar.copy(kn_hi[:, cols], bank[:])
                    if kind == "q":
                        for s in range(2):
                            rows = slice(s * HD_B, (s + 1) * HD_B)
                            last = nc.scalar.copy(q2[rows, a % 2, s, cols], bank[rows, :])
                    if kind == "v":
                        last = nc.scalar.copy(v2[:, 2 * i:2 * i + 2, :, 0:HD_B], bank[:].rearrange("p (t h e) -> p t h e", t=2, h=4))
                    last.then_inc(job_hi, 1)

                def exps(b, k, t, fresh):
                    keys = (2 * unit(k)[1] + t + 1) * P
                    act.wait_ge(nmx_done, (b * UNITS + k) * 2 + (t + 1))
                    if not fresh:
                        act.wait_ge(pt_ready, banks_before(*before(b, k)))
                    nc.scalar.activation(prob[:, k % 2, t, 0:keys], s_ps[t][:, 0:keys], ACT.Exp, bias=nmx[:, k % 2, t:t + 1],
                                         scale=SCALE_B, accum_out=psum_of[:, k % 2, t:t + 1]).then_inc(exp_done, 1)

                def split_pt(b, k, i):
                    act.wait_ge(pt_ready, banks_before(b, k) + (i + 1))
                    nc.scalar.copy(pt_hi[:, 2 * i:2 * i + 2, :], bank_of(k, i)[:]).then_inc(pt_hi_done, 1)

                def out(b, k, fresh):
                    K = b * UNITS + k
                    u = unit(k)[1]
                    s = unit(k)[0] % 2
                    rows = slice(s * HD_B, (s + 1) * HD_B)
                    act.wait_ge(pv_done, K + 1)
                    if s == 0 and not fresh:
                        act.wait_ge(o_done, b * (NPAIR * NU) + (unit(k)[0] // 2 - 1) * NU + (u + 1))
                    nc.scalar.copy(oa[rows, u, :], o_ps[0:HD_B, 0:2 * P]).then_inc(o_out, 1)
                    nc.scalar.copy(ob[rows, u, :], o_ps[HD_B:P, 0:2 * P]).then_inc(o_out, 1)
                    nc.scalar.copy(rb[rows, u, :], o_ps[rows, 2 * P:]).then_inc(o_out, 1)

                norm(0)
                act.wait_ge(zeroed, 2)
                act.wait_ge(small_in, 48)
                nc.scalar.copy(bo[0:1, :], bo_raw).then_inc(w_hi_done, 1)
                act.wait_ge(w_in, 32)
                nc.scalar.copy(w_hi[:].rearrange("p d n -> p (d n)"), w_raw[:, :WQKV]).then_inc(w_hi_done, 1)
                for i, j in enumerate(PRO):
                    job(-1, j, i, True, pro_ps[i % 4])
                    if i == DB - 1:
                        norm(1)
                        nc.scalar.copy(wo_hi[:].rearrange("p g n -> p (g n)"), w_raw[:, WQKV:]).then_inc(w_hi_done, 1)
                act.wait_ge(w_lo_done, 3)
                for t in range(2):
                    exps(0, 0, t, True)

                def body(b, first, last):
                    steps, _ = plan(b, first, last)
                    for k in range(UNITS):
                        early, late = steps[k]
                        more = not (last and k == UNITS - 1)
                        u = unit(k)[1]
                        pu = unit(before(b, k)[1])[1] if not (first and k == 0) else -1
                        for i in range(max(u, pu) + 1):
                            for what in ACT_ORDER[u][i] if i <= u else "":
                                if what == "h":
                                    split_pt(b, k, i)
                                elif more:
                                    exps(*after(b, k), int(what), first and k == 0)
                            if early and i == JOB_AFTER[unit(k)[1]]:
                                job(b, *early[:2])
                            if i == pu and not OUT_LATE[u]:
                                out(*before(b, k), first and k <= 2 * NU)
                        if OUT_LATE[u] and pu >= 0:
                            out(*before(b, k), first and k <= 2 * NU)
                        if late:
                            job(b, *late[:2])
                        if not last and k in NORM_AT:
                            norm((b + 1) * BC + NORM_AT.index(k))

                sequences(act, body)
                out(B - 1, UNITS - 1, False)

            @block.vector
            def _(dve):
                def ln_stats(n, fresh):
                    if not fresh:
                        dve.wait_ge(rstd_done, n)
                    for j in range(CT):
                        nc.vector.bn_stats(stats[:, j, :], x_sb[:, dyn(n * CT + j), :]).then_inc(stats_done, 1)
                    wait_apart(nc, dve, c, stats_done, n * CT + CT)
                    for j in range(CT):
                        nc.vector.bn_aggr(mv[:, j, :], stats[:, j, :]).then_inc(mv_done, 1)

                def job(b, j, number, split_number, bank=j_ps):
                    kind, a, i = j
                    if kind == "y":
                        dve.wait_ge(j_ready, number + 1)
                    else:
                        dve.wait_ge(job_hi, split_number + 1)
                    cols = slice(i * CW, (i + 1) * CW)
                    if kind == "x":
                        last = nc.vector.tensor_tensor(xt_lo[:, a, i, :], bank[:], xt_hi[:, a, i, :].bitcast(F32), ALU.subtract)
                    if kind == "k":
                        last = nc.vector.tensor_tensor(kn_lo[:, cols], bank[:], kn_hi[:, cols].bitcast(F32), ALU.subtract)
                    if kind == "q":
                        for s in range(2):
                            rows, other = slice(s * HD_B, (s + 1) * HD_B), slice((1 - s) * HD_B, (2 - s) * HD_B)
                            last = nc.vector.tensor_tensor(q2[other, a % 2, s, cols], bank[rows, :], q2[rows, a % 2, s, cols].bitcast(F32), ALU.subtract)
                    if kind == "v":
                        last = nc.vector.tensor_tensor(v2[:, 2 * i:2 * i + 2, :, HD_B:], bank[:].rearrange("p (t h e) -> p t h e", t=2, h=4),
                                                       v2[:, 2 * i:2 * i + 2, :, 0:HD_B].bitcast(F32), ALU.subtract)
                    if kind == "y":
                        xs = x_sb[:, dyn((b if a >= 0 else b - 1) * BT + 2 * i, 2), :]
                        last = nc.vector.tensor_tensor(xs, bank[:].rearrange("p (t d) -> p t d", t=2), xs, ALU.add)
                    last.then_inc(j_done, 1)

                def maxima(b, k, t):
                    K = b * UNITS + k
                    h, u = unit(k)
                    tile = 2 * u + t
                    done = (K * 2 + t) * 2
                    far = max(tile - 1, 0) * P
                    near = slice(far, (tile + 1) * P)
                    dve.wait_ge(s_ready, K * 2 + (t + 1))
                    if far:
                        nc.vector.tensor_reduce(mx[:, t, 1:2], s_ps[t][:, 0:far], AX.X, ALU.max).then_inc(mx_step, 1)
                    else:
                        nc.vector.memset(mx[:, t, 1:2], LOWEST).then_inc(mx_step, 1)
                    nc.vector.tensor_tensor_reduce(out=s_ps[t][:, near], in0=s_ps[t][:, near], in1=bias[:, h, NEAR - (tile + 1) * P + far:], op0=ALU.add,
                                                   op1=ALU.max, scale=1.0, scalar=LOWEST, accum_out=mx[:, t, 0:1]).then_inc(mx_step, 1)
                    dve.wait_ge(mx_step, done + 2)
                    nc.vector.tensor_scalar(nmx[:, k % 2, t:t + 1], mx[:, t, 0:1], mx[:, t, 1:2], -SCALE_B, ALU.max, ALU.mult).then_inc(nmx_done, 1)

                def reciprocals(b, k, fresh):
                    if not fresh:
                        dve.wait_ge(pv_done, b * UNITS + k - 1)
                    dve.wait_ge(exp_done, (b * UNITS + k) * 2 + 2)
                    nc.vector.reciprocal(rsum[:, k % 2, :], psum_of[:, k % 2, :]).then_inc(rsum_done, 1)

                def split_pt(b, k, i):
                    dve.wait_ge(pt_hi_done, banks_before(b, k) + (i + 1))
                    nc.vector.tensor_tensor(pt_lo[:, 2 * i:2 * i + 2, :], bank_of(k, i)[:], pt_hi[:, 2 * i:2 * i + 2, :].bitcast(F32),
                                            ALU.subtract).then_inc(pt_lo_done, 1)

                nc.vector.memset(bo[:].bitcast(F32), 0.0).then_inc(zeroed, 1)
                nc.vector.memset(pick[:].bitcast(F32), 0.0).then_inc(zeroed, 1)
                nc.vector.memset(zeros[:], 0.0).then_inc(set_up, 1)
                ln_stats(0, True)
                dve.wait_ge(zeroed, 2)
                for r in (0, 32):
                    last = nc.vector.memset(pick[r:r + 1, :].bitcast(F32), 1.0)
                last.then_inc(set_up, 1)
                dve.wait_ge(small_in, 48)
                nc.vector.tensor_copy(rel_wide, rel[:].unsqueeze(2).to_broadcast([BUCKETS + 1, H_B, P])).then_inc(rel_done, 1)
                dve.wait_ge(w_hi_done, 1)
                nc.vector.tensor_tensor(bo[32:33, :], bo_raw, bo[0:1, :].bitcast(F32), ALU.subtract).then_inc(w_lo_done, 1)
                ln_stats(1, False)
                for h in range(H_B):
                    lo = (h // 2 % 2) * CW
                    dve.wait_ge(band_ready, h + 1)
                    nc.vector.tensor_copy(band[h], s_ps[h % 2][:, lo:lo + SPAN]).then_inc(band_done, 1)
                    if h == 3:
                        for i in range(DB):
                            job(-1, PRO[i], i, i, pro_ps[i])
                        dve.wait_ge(w_hi_done, 2)
                        nc.vector.tensor_tensor(w_lo[:].rearrange("p d n -> p (d n)"), w_raw[:, :WQKV], w_hi[:].bitcast(F32).rearrange("p d n -> p (d n)"),
                                                ALU.subtract).then_inc(w_lo_done, 1)
                for i in range(DB, len(PRO)):
                    job(-1, PRO[i], i, i, pro_ps[i % 4])
                dve.wait_ge(bias_in, 16 * H_B)
                for t in range(2):
                    maxima(0, 0, t)

                def body(b, first, last):
                    steps, _ = plan(b, first, last)
                    for k in range(UNITS):
                        early, late = steps[k]
                        reciprocals(b, k, first and k < 2)
                        for i in range(unit(k)[1] + 1):
                            for what in DVE_ORDER[unit(k)[1]][i]:
                                if what == "l":
                                    split_pt(b, k, i)
                                elif not (last and k == UNITS - 1):
                                    maxima(*after(b, k), int(what))
                            if early and i == JOB_AFTER[unit(k)[1]]:
                                job(b, *early)
                        if late:
                            job(b, *late)
                        if not last and k in STATS_AT:
                            ln_stats((b + 1) * BC + STATS_AT.index(k), False)

                sequences(dve, body)
                for j, number in TAIL:
                    job(B - 1, j, number, None)

            @block.gpsimd
            def _(pool):
                def ln_rstd(n, fresh):
                    if not fresh:
                        pool.wait_ge(xn_done, n * CT)
                    pool.wait_ge(mv_done, n * CT + CT)
                    nc.gpsimd.tensor_tensor(veps[:], mv[:, :, 1], c.eps[:], ALU.add).then_inc(pool_step, 1)
                    pool.wait_ge(pool_step, n * 3 + 1)
                    nc.gpsimd.tensor_tensor(rstd[:], veps[:], c.minus_half[:], ALU.pow).then_inc(pool_step, 1)
                    pool.wait_ge(pool_step, n * 3 + 2)
                    nc.gpsimd.tensor_tensor(mr[:], mv[:, :, 0], rstd[:], ALU.mult).then_inc(pool_step, 1)
                    pool.wait_ge(pool_step, n * 3 + 3)
                    nc.gpsimd.tensor_tensor(nmr[:], mr[:], c.minus_one[:], ALU.mult).then_inc(rstd_done, 1)

                def combine(b, k, y_number):
                    u = unit(k)[1]
                    G = b * (NPAIR * NU) + (k // (2 * NU) * NU + u)
                    cols = slice(u * 2 * P, (u + 1) * 2 * P)
                    pool.wait_ge(o_out, (b * UNITS + k) * 3 + 3)
                    if not (isinstance(G, int) and G == 0):
                        pool.wait_ge(o_done, G)
                    nc.gpsimd.tensor_tensor(osum[:], oa[:, u, :], ob[:, u, :], ALU.add).then_inc(o_step, 1)
                    pool.wait_ge(o_step, G * 3 + 1)
                    nc.gpsimd.tensor_tensor(oa[:, u, :], osum[:], rb[:, u, :], ALU.mult).then_inc(o_step, 1)
                    pool.wait_ge(o_step, G * 3 + 2)
                    if y_number is not None:
                        pool.wait_ge(j_ready, y_number + 1)
                    nc.gpsimd.tensor_tensor(carrier[:], c.eps[:, 0:1], c.eps[:, 0:1], ALU.add)
                    nc.gpsimd.tensor_scalar(o_hi[:, cols], oa[:, u, :], 1.0, 1.0, ALU.mult, ALU.mult).then_inc(o_step, 1)
                    pool.wait_ge(o_step, G * 3 + 3)
                    nc.gpsimd.tensor_tensor(o_lo[:, cols], oa[:, u, :], o_hi[:, cols].bitcast(F32), ALU.subtract).then_inc(o_done, 1)

                ln_rstd(0, True)
                ln_rstd(1, False)
                pool.wait_ge(w_hi_done, 3)
                nc.gpsimd.tensor_tensor(wo_lo[:].rearrange("p g n -> p (g n)"), w_raw[:, WQKV:], wo_hi[:].bitcast(F32).rearrange("p g n -> p (g n)"),
                                        ALU.subtract).then_inc(w_lo_done, 1)

                def body(b, first, last):
                    _, number = plan(b, first, last)

                    for k in range(UNITS):
                        pb, pk = before(*before(b, k))
                        if unit(pk)[0] % 2 and not (first and k < 2):
                            p, u = pk // (2 * NU) if k >= 2 else -1, unit(pk)[1]
                            combine(pb, pk, None if first and p == 0 else number["y", p - 1, u])
                        if not last and k in RSTD_AT:
                            ln_rstd((b + 1) * BC + RSTD_AT.index(k), False)

                sequences(pool, body)
                for k in (UNITS - 2, UNITS - 1):
                    combine(B - 1, k, LAST_NUMBER["y", NPAIR - 2, unit(k)[1]])

        m.clear_sems()


class Consts:
    pass


def build(nc, dram):
    x_view = dram["x"].rearrange("(t p) d -> p t d", p=P)
    out_view = dram["out"].rearrange("(t p) d -> p t d", p=P)
    with ExitStack() as ctx:
        m = Mem(nc, ctx, "all")
        x_sb = m.sb("x", [P, T, D])
        c = Consts()
        c.ident = m.sb("ident", [P, P])
        c.iota8 = m.sb("iota8", [P, E])
        c.minus_half = m.sb("minus_half", [P, CT])
        c.minus_one = m.sb("minus_one", [P, CT])
        c.eps = m.sb("eps", [P, CT])
        c.carrier = m.sb("carrier", [P, 1])
        loaded = m.sem("loaded")
        made = m.sem("made")
        with nc.Block() as block:

            @block.sync
            def _(sp):
                sp.dma_start(c.ident[:], dram["ident"]).then_inc(loaded, 16)
                sp.dma_start(c.iota8[:], dram["iota8"]).then_inc(loaded, 16)
                sp.dma_start(x_sb[:, 0:BT, :], x_view[:, 0:BT, :]).then_inc(loaded, 16)
                sp.wait_ge(loaded, 16 * 3)

            @block.vector
            def _(dve):
                for tile, value in ((c.minus_half, -0.5), (c.minus_one, -1.0), (c.eps, EPS_LN)):
                    nc.vector.memset(tile[:], value).then_inc(made, 1)
                dve.wait_ge(made, 3)

        linear_attention_stage(nc, x_sb, c, dram)
        ffn_stage(nc, "f1", x_sb, c, dram)
        softmax_attention_stage(nc, x_sb, c, dram)
        ffn_stage(nc, "f2", x_sb, c, dram, out_view)


def by_dist():
    n = NEAR - 1 - np.arange(SPAN)
    exact = BUCKETS // 2
    large = exact + (np.log(np.maximum(n, 1).astype(np.float32) / np.float32(exact)) / np.float32(math.log(MAX_DIST / exact))
                     * np.float32(BUCKETS - exact)).astype(np.int32)
    bucket = np.where(n < exact, np.maximum(n, 0), np.minimum(large, BUCKETS - 1))
    table = np.zeros((BUCKETS + 1, SPAN), np.float32)
    for col in range(SPAN):
        if n[col] >= 0:
            table[bucket[col], col] += 1 / SCALE_B ** 2
            table[BUCKETS - 1, col] -= 1 / SCALE_B ** 2
        else:
            table[BUCKETS, col] = MASKED
    return table


def layouts(v):
    a = {k: np.asarray(x) for k, x in v.items()}
    gate, up, downw = a["L0_ffn_Wg"], a["L0_ffn_Wu"], a["L0_ffn_Wd"]
    w_ffn = np.empty((NFB, P, FBW), np.float32)
    for fb in range(NFB):
        if fb < NSH:
            cols = slice(fb * F, (fb + 1) * F)
            g, u, d = a["L0_ffn_Sg"][:, cols], a["L0_ffn_Su"][:, cols], a["L0_ffn_Sd"][cols]
        else:
            g, u, d = gate[fb - NSH], up[fb - NSH], downw[fb - NSH]
        for k in range(DB):
            w_ffn[fb, :, k * 2 * F:k * 2 * F + F] = g[k * P:(k + 1) * P]
            w_ffn[fb, :, k * 2 * F + F:(k + 1) * 2 * F] = u[k * P:(k + 1) * P]
        w_ffn[fb, :, 2 * D:] = d
    out = {
        "x": a["L0_attn_a_x"].reshape(B * N, D),
        "w_qkv_a": np.concatenate([a[f"L0_attn_a_W{k}"].T.reshape(DB, P, D).transpose(1, 0, 2) for k in "qkv"], axis=2),
        "b_q_a": a["L0_attn_a_bq"].reshape(DB, P).T,
        "b_kv_a": np.concatenate([a["L0_attn_a_bk"], a["L0_attn_a_bv"]]).reshape(1, 2 * D),
        "gamma": a["L0_attn_a_gamma"].reshape(1, D),
        "beta": a["L0_attn_a_beta"].reshape(1, D),
        "head_mask": np.kron(np.eye(HB_A, dtype=np.float32), np.ones((HD_A, HD_A), np.float32)),
        "head_of": np.kron(np.eye(HB_A, dtype=np.float32), np.ones((HD_A, 1), np.float32)),
        "w_qkv_b": np.concatenate([a["L0_attn_b_Wq"], a["L0_attn_b_Wkv"]], axis=1).reshape(DB, P, 3 * INNER).transpose(1, 0, 2).reshape(P, -1),
        "w_o_b": a["L0_attn_b_Wo"].reshape(NPAIR, P, D).transpose(1, 0, 2).reshape(P, -1),
        "b_o_b": np.tile(a["L0_attn_b_bo"].reshape(1, D), (1, 2)),
        "rel_emb": np.concatenate([a["L0_attn_b_rel_emb"], np.ones((1, H_B), np.float32)]),
        "by_dist": by_dist(),
        "w_ffn": w_ffn,
        "w_router": a["L0_ffn_Wr"].reshape(DB, P, E).transpose(1, 0, 2),
        "expert_bias": a["L0_ffn_expert_bias"].reshape(E, 1),
        "ident": np.eye(P, dtype=np.float32),
        "iota8": np.tile(np.arange(E, dtype=np.float32), (P, 1)),
    }
    return {k: np.ascontiguousarray(x) for k, x in out.items()}


def kernel(**inputs):
    import concourse.bacc as bacc
    from concourse.bass_utils import run_bass_kernel_spmd

    nc = bacc.Bacc("TRN2", target_bir_lowering=False, num_devices=1)
    arrays = {f"in_{k}": x for k, x in layouts(inputs).items()}
    dram = {k[3:]: nc.dram_tensor(k, x.shape, mybir.dt.from_np(x.dtype), kind="ExternalInput").ap() for k, x in arrays.items()}
    dram["out"] = nc.dram_tensor("out", (B * N, D), F32, kind="ExternalOutput").ap()
    build(nc, dram)
    r = run_bass_kernel_spmd(nc, [arrays], core_ids=[0])
    return r.results[0]["out"].reshape(B, N, D)
```
